# Optimizing a Trainium2 kernel written in Bass

```python
import numpy as np
import jax
import jax.numpy as jnp

def _softmax(x, axis=-1):
    return jax.nn.softmax(x, axis=axis)

def _gelu(x):
    return jax.nn.gelu(x, approximate=True)

def _silu(x):
    return jax.nn.silu(x)

def _sigmoid(x):
    return jax.nn.sigmoid(x)

def _layernorm(x, axis=-1, eps=1e-05):
    m = jnp.mean(x, axis=axis, keepdims=True)
    v = jnp.var(x, axis=axis, keepdims=True)
    return (x - m) / jnp.sqrt(v + eps)

def _scatter_add(tgt, idx, src, axis=0):
    return tgt.at[idx].add(src)

def _segment_sum(src, seg, n):
    return jax.ops.segment_sum(src, seg, n)
kernel_name = 'mk_xattn_ffn_d1_seqx_r8_87b6b1'

def setup_inputs(seed: int=0):
    np.random.seed(seed)
    _w = jnp.asarray

    def _rec_inputs():
        import jax
        import jax.numpy as jnp
        _rk = jax.random.key(seed)
        x = 7.22e-05 + 1 * jax.random.normal(jax.random.fold_in(_rk, 1), (32, 128, 128), jnp.float32)
        _lenS = 128 - jax.random.randint(jax.random.fold_in(_rk, 7), (32,), 0, max(1, 128 // 4) + 1, jnp.int32)
        _lenS2 = 128 - jax.random.randint(jax.random.fold_in(_rk, 8), (32,), 0, max(1, 128 // 4) + 1, jnp.int32)
        _ctx_1024P = jax.random.normal(jax.random.fold_in(_rk, 11), (32, 16, 128), jnp.float32)
        _ctx_1024c = jax.random.dirichlet(jax.random.fold_in(_rk, 511), 0.3 * jnp.ones((16,), jnp.float32), (32, 128))
        _ctx_1024t = jnp.einsum('bsk,bkd->bsd', _ctx_1024c, _ctx_1024P)
        _ctx_1024t = _ctx_1024t * jax.lax.rsqrt(jnp.mean(jnp.square(_ctx_1024t)) + 1e-12) * 0.953939
        ctx_1024 = 4.13588e-05 + 0.999923 * (_ctx_1024t + 0.3 * jax.random.normal(jax.random.fold_in(_rk, 611), (32, 128, 128), jnp.float32))
        fside_BxS2_0 = jax.random.uniform(jax.random.fold_in(_rk, 12), (32, 128), jnp.float32, 0.0, 0.999833)
        _validS = jnp.arange(128)[None, :] < _lenS[:, None]
        _validS2 = jnp.arange(128)[None, :] < _lenS2[:, None]
        _causal = jnp.tril(jnp.ones((128, 128), dtype=bool))
        mask_BxS2_ff1 = jnp.where(jnp.ones((32, 128), dtype=bool), 1.0, 0.0).astype(jnp.float32)
        return (x, ctx_1024, fside_BxS2_0, mask_BxS2_ff1)
    x, ctx_1024, fside_BxS2_0, mask_BxS2_ff1 = _rec_inputs()

    def _L0_xattn_setup():
        import jax, jax.numpy as jnp
        import numpy as np
        EMBED_DIM = 128
        NUM_HEADS = 16
        NUM_KV = 4
        KEY_DIM = EMBED_DIM // NUM_HEADS
        SCALE = 1.0 / float(KEY_DIM) ** 0.5
        key = jax.random.key(seed)
        ks = jax.random.split(key, 10)
        B, S, E = (4, 256, EMBED_DIM)
        kv_dim = KEY_DIM * NUM_KV
        return {'query': jax.random.normal(ks[0], (B, S, E), dtype=jnp.float32), 'key': jax.random.normal(ks[1], (B, S, E), dtype=jnp.float32), 'value': jax.random.normal(ks[2], (B, S, E), dtype=jnp.float32), 'session_deltas': jax.random.uniform(ks[3], (B, S), dtype=jnp.float32), 'mask': jnp.ones((B, S), dtype=jnp.float32), 'Wq': jax.random.normal(ks[4], (E, E), dtype=jnp.float32) * E ** (-0.5), 'Wk': jax.random.normal(ks[5], (E, kv_dim), dtype=jnp.float32) * E ** (-0.5), 'Wv': jax.random.normal(ks[6], (E, kv_dim), dtype=jnp.float32) * E ** (-0.5), 'Wo': jax.random.normal(ks[7], (E, E), dtype=jnp.float32) * E ** (-0.5), 'time_bias_weight': jax.random.normal(ks[8], ()) * 0.01}
    _L0_xattn_all = _L0_xattn_setup()
    _L0_xattn_in = {k: v for k, v in _L0_xattn_all.items() if k in ('Wq', 'Wk', 'Wv', 'Wo', 'time_bias_weight')}
    del _L0_xattn_all

    def _L0_ffn_setup():
        import jax, jax.numpy as jnp
        import numpy as np
        DIM = 128
        DEPTH = 6
        HEADS = 16
        DIM_HEAD = 64
        WINDOW = 32
        INNER = HEADS * DIM_HEAD
        DIM_INNER = int(DIM * 4 * 2 / 3)
        QK_SCALE = 8.0

        def shift_tokens(t):
            a, s = jnp.split(t, 2, -1)
            s = jnp.pad(s, ((0, 0), (1, 0), (0, 0)))[:, :-1]
            return jnp.concatenate([a, s], -1)

        def l2norm(t):
            return t / jnp.maximum(jnp.linalg.norm(t, axis=-1, keepdims=True), 1e-12)

        def rotate_half(x):
            x1, x2 = jnp.split(x, 2, -1)
            return jnp.concatenate([-x2, x1], -1)

        def rotary_tables(n):
            half = jnp.arange(0, DIM_HEAD, 2, dtype=jnp.float32)
            inv_freq = 1.0 / 10000.0 ** (half / DIM_HEAD)
            t = jnp.arange(n, dtype=jnp.float32)
            freqs = t[:, None] * inv_freq[None, :]
            freqs = jnp.concatenate([freqs, freqs], -1)
            base_scale = (half + 0.4 * DIM_HEAD) / (1.4 * DIM_HEAD)
            power = (t - n // 2) / (WINDOW // 2)
            scale = base_scale[None, :] ** power[:, None]
            scale = jnp.concatenate([scale, scale], -1)
            return (freqs, scale)

        def local_attention(q, k, v):
            b, h, n, d = q.shape
            w = WINDOW
            nw = n // w
            bq = q.reshape(b, h, nw, w, d)
            bk = k.reshape(b, h, nw, w, d)
            bv = v.reshape(b, h, nw, w, d)

            def look(t):
                p = jnp.pad(t, ((0, 0), (0, 0), (1, 0), (0, 0), (0, 0)))
                return jnp.concatenate([p[:, :, :nw], p[:, :, 1:]], axis=3)
            bk2, bv2 = (look(bk), look(bv))
            seq = jnp.arange(n).reshape(nw, w)
            seq_p = jnp.pad(seq, ((1, 0), (0, 0)), constant_values=-1)
            jt = jnp.concatenate([seq_p[:nw], seq_p[1:]], axis=1)
            it = seq[:, :, None]
            jb = jt[:, None, :]
            mask = (it < jb) | (it > jb + w) | (jb == -1)
            sim = jnp.einsum('bhwie,bhwje->bhwij', bq, bk2) * QK_SCALE
            sim = jnp.where(mask, -jnp.finfo(sim.dtype).max, sim)
            attn = jax.nn.softmax(sim, -1)
            out = jnp.einsum('bhwij,bhwje->bhwie', attn, bv2)
            return out.reshape(b, h, n, d)

        def attn_layer(x, Wqkv, qs, ksc, Wo):
            b, n, _ = x.shape
            qkv = x @ Wqkv
            q, k, v = jnp.split(qkv, 3, -1)
            sh = lambda t: t.reshape(b, n, HEADS, DIM_HEAD).transpose(0, 2, 1, 3)
            q, k, v = (sh(q), sh(k), sh(v))
            q = l2norm(q) * qs
            k = l2norm(k) * ksc
            freqs, scale = rotary_tables(n)
            cos, sin = (jnp.cos(freqs), jnp.sin(freqs))
            q = q * cos * scale + rotate_half(q) * sin * scale
            inv = 1.0 / scale
            k = k * cos * inv + rotate_half(k) * sin * inv
            out = local_attention(q, k, v)
            out = out.transpose(0, 2, 1, 3).reshape(b, n, INNER)
            return out @ Wo

        def ffn_layer(x, g, bln, W1, b1, W2, b2):
            mu = x.mean(-1, keepdims=True)
            var = ((x - mu) ** 2).mean(-1, keepdims=True)
            xn = (x - mu) / jnp.sqrt(var + 1e-05) * g + bln
            hg = xn @ W1 + b1
            a, gate = jnp.split(hg, 2, -1)
            return a * jax.nn.gelu(gate, approximate=False) @ W2 + b2
        key = jax.random.key(seed)
        ks = jax.random.split(key, 8)
        B, N = (2, 256)
        init = lambda k, shape: jax.random.normal(k, shape, jnp.float32) * 0.02
        return {'x': jax.random.normal(ks[0], (B, N, DIM), jnp.float32), 'Wqkv': init(ks[1], (DEPTH, DIM, 3 * INNER)), 'q_scale': jnp.ones((DEPTH, DIM_HEAD), jnp.float32), 'k_scale': jnp.ones((DEPTH, DIM_HEAD), jnp.float32), 'Wo': init(ks[2], (DEPTH, INNER, DIM)), 'ln_g': jnp.ones((DEPTH, DIM), jnp.float32), 'ln_b': jnp.zeros((DEPTH, DIM), jnp.float32), 'W1': init(ks[3], (DEPTH, DIM, 2 * DIM_INNER)), 'b1': jnp.zeros((DEPTH, 2 * DIM_INNER), jnp.float32), 'W2': init(ks[4], (DEPTH, DIM_INNER, DIM)), 'b2': jnp.zeros((DEPTH, DIM), jnp.float32)}
    _L0_ffn_all = _L0_ffn_setup()
    _L0_ffn_in = {k: v for k, v in _L0_ffn_all.items() if k in ('Wqkv', 'q_scale', 'k_scale', 'Wo', 'ln_g', 'ln_b', 'W1', 'b1', 'W2', 'b2')}
    del _L0_ffn_all
    return {'x': x, 'ctx_1024': ctx_1024, 'fside_BxS2_0': fside_BxS2_0, 'mask_BxS2_ff1': mask_BxS2_ff1, 'L0_xattn_Wq': _L0_xattn_in['Wq'], 'L0_xattn_Wk': _L0_xattn_in['Wk'], 'L0_xattn_Wv': _L0_xattn_in['Wv'], 'L0_xattn_Wo': _L0_xattn_in['Wo'], 'L0_xattn_time_bias_weight': _L0_xattn_in['time_bias_weight'], 'L0_ffn_Wqkv': _L0_ffn_in['Wqkv'], 'L0_ffn_q_scale': _L0_ffn_in['q_scale'], 'L0_ffn_k_scale': _L0_ffn_in['k_scale'], 'L0_ffn_Wo': _L0_ffn_in['Wo'], 'L0_ffn_ln_g': _L0_ffn_in['ln_g'], 'L0_ffn_ln_b': _L0_ffn_in['ln_b'], 'L0_ffn_W1': _L0_ffn_in['W1'], 'L0_ffn_b1': _L0_ffn_in['b1'], 'L0_ffn_W2': _L0_ffn_in['W2'], 'L0_ffn_b2': _L0_ffn_in['b2']}

def reference(x, ctx_1024, fside_BxS2_0, mask_BxS2_ff1, L0_xattn_Wq, L0_xattn_Wk, L0_xattn_Wv, L0_xattn_Wo, L0_xattn_time_bias_weight, L0_ffn_Wqkv, L0_ffn_q_scale, L0_ffn_k_scale, L0_ffn_Wo, L0_ffn_ln_g, L0_ffn_ln_b, L0_ffn_W1, L0_ffn_b1, L0_ffn_W2, L0_ffn_b2):
    import jax
    import jax.numpy as jnp

    def _L0_xattn_ref(query, key, value, session_deltas, mask, Wq, Wk, Wv, Wo, time_bias_weight):
        import jax, jax.numpy as jnp
        import numpy as np
        EMBED_DIM = 128
        NUM_HEADS = 16
        NUM_KV = 4
        KEY_DIM = EMBED_DIM // NUM_HEADS
        SCALE = 1.0 / float(KEY_DIM) ** 0.5
        B, S, E = query.shape
        H, G, D = (NUM_HEADS, NUM_KV, KEY_DIM)
        n_rep = H // G
        q = (query @ Wq).reshape(B, S, H, D).transpose(0, 2, 1, 3)
        k = (key @ Wk).reshape(B, S, G, D).transpose(0, 2, 1, 3)
        v = (value @ Wv).reshape(B, S, G, D).transpose(0, 2, 1, 3)
        k_rep = jnp.repeat(k, n_rep, axis=1)
        v_rep = jnp.repeat(v, n_rep, axis=1)
        scores = jnp.einsum('bhqd,bhkd->bhqk', q, k_rep) * SCALE
        ct = jnp.cumsum(session_deltas, axis=1)
        pairwise_delta = jnp.abs(ct[:, :, None] - ct[:, None, :])
        time_bias = time_bias_weight * jnp.log1p(pairwise_delta)
        scores = scores + time_bias[:, None, :, :]
        scores = scores + (1.0 - mask[:, None, None, :].astype(scores.dtype)) * -1000000000.0
        w = jax.nn.softmax(scores, axis=-1)
        out = jnp.einsum('bhqk,bhkd->bhqd', w, v_rep)
        out = out.transpose(0, 2, 1, 3).reshape(B, S, E)
        return out @ Wo

    def _L0_ffn_ref(x, Wqkv, q_scale, k_scale, Wo, ln_g, ln_b, W1, b1, W2, b2):
        import jax, jax.numpy as jnp
        import numpy as np
        DIM = 128
        DEPTH = 6
        HEADS = 16
        DIM_HEAD = 64
        WINDOW = 32
        INNER = HEADS * DIM_HEAD
        DIM_INNER = int(DIM * 4 * 2 / 3)
        QK_SCALE = 8.0

        def shift_tokens(t):
            a, s = jnp.split(t, 2, -1)
            s = jnp.pad(s, ((0, 0), (1, 0), (0, 0)))[:, :-1]
            return jnp.concatenate([a, s], -1)

        def l2norm(t):
            return t / jnp.maximum(jnp.linalg.norm(t, axis=-1, keepdims=True), 1e-12)

        def rotate_half(x):
            x1, x2 = jnp.split(x, 2, -1)
            return jnp.concatenate([-x2, x1], -1)

        def rotary_tables(n):
            half = jnp.arange(0, DIM_HEAD, 2, dtype=jnp.float32)
            inv_freq = 1.0 / 10000.0 ** (half / DIM_HEAD)
            t = jnp.arange(n, dtype=jnp.float32)
            freqs = t[:, None] * inv_freq[None, :]
            freqs = jnp.concatenate([freqs, freqs], -1)
            base_scale = (half + 0.4 * DIM_HEAD) / (1.4 * DIM_HEAD)
            power = (t - n // 2) / (WINDOW // 2)
            scale = base_scale[None, :] ** power[:, None]
            scale = jnp.concatenate([scale, scale], -1)
            return (freqs, scale)

        def local_attention(q, k, v):
            b, h, n, d = q.shape
            w = WINDOW
            nw = n // w
            bq = q.reshape(b, h, nw, w, d)
            bk = k.reshape(b, h, nw, w, d)
            bv = v.reshape(b, h, nw, w, d)

            def look(t):
                p = jnp.pad(t, ((0, 0), (0, 0), (1, 0), (0, 0), (0, 0)))
                return jnp.concatenate([p[:, :, :nw], p[:, :, 1:]], axis=3)
            bk2, bv2 = (look(bk), look(bv))
            seq = jnp.arange(n).reshape(nw, w)
            seq_p = jnp.pad(seq, ((1, 0), (0, 0)), constant_values=-1)
            jt = jnp.concatenate([seq_p[:nw], seq_p[1:]], axis=1)
            it = seq[:, :, None]
            jb = jt[:, None, :]
            mask = (it < jb) | (it > jb + w) | (jb == -1)
            sim = jnp.einsum('bhwie,bhwje->bhwij', bq, bk2) * QK_SCALE
            sim = jnp.where(mask, -jnp.finfo(sim.dtype).max, sim)
            attn = jax.nn.softmax(sim, -1)
            out = jnp.einsum('bhwij,bhwje->bhwie', attn, bv2)
            return out.reshape(b, h, n, d)

        def attn_layer(x, Wqkv, qs, ksc, Wo):
            b, n, _ = x.shape
            qkv = x @ Wqkv
            q, k, v = jnp.split(qkv, 3, -1)
            sh = lambda t: t.reshape(b, n, HEADS, DIM_HEAD).transpose(0, 2, 1, 3)
            q, k, v = (sh(q), sh(k), sh(v))
            q = l2norm(q) * qs
            k = l2norm(k) * ksc
            freqs, scale = rotary_tables(n)
            cos, sin = (jnp.cos(freqs), jnp.sin(freqs))
            q = q * cos * scale + rotate_half(q) * sin * scale
            inv = 1.0 / scale
            k = k * cos * inv + rotate_half(k) * sin * inv
            out = local_attention(q, k, v)
            out = out.transpose(0, 2, 1, 3).reshape(b, n, INNER)
            return out @ Wo

        def ffn_layer(x, g, bln, W1, b1, W2, b2):
            mu = x.mean(-1, keepdims=True)
            var = ((x - mu) ** 2).mean(-1, keepdims=True)
            xn = (x - mu) / jnp.sqrt(var + 1e-05) * g + bln
            hg = xn @ W1 + b1
            a, gate = jnp.split(hg, 2, -1)
            return a * jax.nn.gelu(gate, approximate=False) @ W2 + b2
        for i in range(DEPTH):
            x = attn_layer(shift_tokens(x), Wqkv[i], q_scale[i], k_scale[i], Wo[i]) + x
            x = ffn_layer(shift_tokens(x), ln_g[i], ln_b[i], W1[i], b1[i], W2[i], b2[i]) + x
        return x
    x = x + _L0_xattn_ref(_layernorm(x, axis=-1), ctx_1024, ctx_1024, fside_BxS2_0, mask_BxS2_ff1, L0_xattn_Wq, L0_xattn_Wk, L0_xattn_Wv, L0_xattn_Wo, L0_xattn_time_bias_weight)
    x = x + _L0_ffn_ref(_layernorm(x, axis=-1), L0_ffn_Wqkv, L0_ffn_q_scale, L0_ffn_k_scale, L0_ffn_Wo, L0_ffn_ln_g, L0_ffn_ln_b, L0_ffn_W1, L0_ffn_b1, L0_ffn_W2, L0_ffn_b2)
    return x

_drawn_inputs = setup_inputs


def setup_inputs(seed=0):
    import zlib

    import numpy as np

    out = dict(_drawn_inputs(seed))
    spreads = {'L0_ffn_q_scale': (1.0, 0.6),
     'L0_ffn_k_scale': (1.0, 0.6),
     'L0_ffn_ln_g': (1.0, 0.6),
     'L0_ffn_ln_b': (0.0, 0.8),
     'L0_ffn_b1': (0.0, 0.8),
     'L0_ffn_b2': (0.0, 0.1)}
    factors = {'L0_ffn_W1': 4.348, 'L0_ffn_W2': 4.273}
    for name, (base, spread) in spreads.items():
        noise = np.random.default_rng([zlib.crc32(name.encode()), seed]).standard_normal(out[name].shape)
        drawn = base * np.exp(spread * noise) if base else spread * noise
        out[name] = jnp.asarray(drawn.astype(out[name].dtype))
    for name, factor in factors.items():
        out[name] = (out[name] * factor).astype(out[name].dtype)
    return out
```

```python
from contextlib import ExitStack

import numpy as np

import concourse.bass as bass
from concourse import mybir

F32 = mybir.dt.float32
BF16 = mybir.dt.bfloat16
ALU = mybir.AluOpType
ACT = mybir.ActivationFunctionType
AX = mybir.AxisListType

B, S, E = 32, 128, 128
XH, XG, XD = 16, 4, 8
XR = XH // XG
XSCALE = 1.0 / float(XD) ** 0.5
DEPTH, HEADS, DH, WIN = 6, 16, 64, 32
INNER = HEADS * DH
PAIRS = HEADS // 2
NW = S // WIN
FF = int(E * 4 * 2 / 3)
FCH = [(0, 128), (128, 128), (256, FF - 256)]
QK_SCALE = 8.0
UNITS = DEPTH * B
LN_EPS = 1e-5
NORM_MIN2 = 1e-24
MASKED = -(2.0 ** 120)

C_ID, C_SH, C_TRI, C_ROT, C_MASK, C_BLK, C_END = 0, 128, 256, 384, 640, 704, 708


def constants():
    c = np.zeros((128, C_END), np.float32)
    r = np.arange(128)
    c[:, C_ID:C_ID + 128] = np.eye(128)
    c[r[:-1], C_SH + 1 + r[:-1]] = 1.0
    c[:, C_TRI:C_TRI + 128] = r[:, None] <= r[None, :]
    half = np.arange(0, DH, 2, dtype=np.float32)
    inv = (1.0 / np.float32(10000.0) ** (half / np.float32(DH))).astype(np.float32)
    t = np.arange(S, dtype=np.float32)
    f = (t[:, None] * inv[None, :]).astype(np.float32)
    base = (half + np.float32(0.4 * DH)) / np.float32(1.4 * DH)
    scale = (base[None, :] ** ((t - S // 2) / (WIN // 2))[:, None]).astype(np.float32)
    cos, sin = np.cos(f).astype(np.float32), np.sin(f).astype(np.float32)
    for k, s in enumerate((scale * np.float32(QK_SCALE), np.float32(1.0) / scale)):
        o = C_ROT + 128 * k
        c[:, o:o + 64] = np.concatenate([cos * s, cos * s], 1)
        c[:, o + 64:o + 128] = np.concatenate([sin * s, -(sin * s)], 1)
    w = r // WIN
    key = np.where(w == 0, 0, (w - 1) * WIN)[:, None] + np.arange(64)[None, :]
    ok = (key <= r[:, None]) & (key + WIN >= r[:, None])
    c[:, C_MASK:C_MASK + 64] = np.where(ok, 0.0, MASKED)
    c[:, C_BLK:C_BLK + XR] = (r[:, None] // XD) % XR == np.arange(XR)[None, :]
    return c


def build(nc, x, ctx, deltas, mask, xWq, xWk, xWv, xWo, xtw, Wqkv, qs, ks, Wo, lng, lnb, W1, b1, W2, b2, consts, out):
    es = ExitStack()
    with es:
        def sb(name, shape, dt=F32):
            return es.enter_context(nc.sbuf_tensor(name, shape, dt))

        def ps(name):
            return es.enter_context(nc.psum_tensor(name, [128, 512], F32))

        def sem(name):
            return es.enter_context(nc.semaphore(name))

        cst = sb("cst", [128, C_END])
        ident = cst[:, C_ID:C_ID + 128]
        shift = cst[:, C_SH:C_SH + 128]
        tri = cst[:, C_TRI:C_TRI + 128]
        rotc = cst[:, C_ROT:C_ROT + 256]
        blk = cst[:, C_BLK:C_BLK + XR]
        identb = sb("identb", [128, 128], BF16)
        maskb = sb("maskb", [128, 64], BF16)
        z_sb = sb("z_sb", [128, B * E])
        x1_sb = sb("x1_sb", [128, B * E])
        zv = z_sb[:, :].rearrange("p (b e) -> p b e", b=B)
        x1v = x1_sb[:, :].rearrange("p (b e) -> p b e", b=B)
        wqkv = sb("wqkv", [128, 3 * INNER])
        wo = sb("wo", [128, PAIRS, E])
        w1 = sb("w1", [128, 2 * FF])
        w2 = sb("w2", [128, 3, E])
        gb = sb("gb", [128, 2])
        b1c = sb("b1c", [128, 6])
        b2r = sb("b2r", [128, E])
        rot = sb("rot", [128, 4 * DH])
        rot_all = sb("rot_all", [128, DEPTH, 4 * DH])
        qks = sb("qks", [128, 2, DEPTH * DH])
        zcur = sb("zcur", [128, 2, E])
        zsT = sb("zsT", [128, 4, S])
        sq = sb("sq", [128, 2 * INNER])
        ta = sb("ta", [128, 2 * INNER])
        tb = sb("tb", [128, 2 * INNER])
        qk = sb("qk", [128, 2, 2 * INNER])
        ss = sb("ss", [128, 2, 2 * HEADS])
        rn = sb("rn", [128, 2, 2 * HEADS])
        half_neg = sb("half_neg", [128, 2 * HEADS])
        qkT = sb("qkT", [128, 2 * PAIRS, S])
        P = sb("P", [128, 2, HEADS * DH])
        rowmax = sb("rowmax", [128, HEADS])
        rowsum = sb("rowsum", [128, 2, HEADS])
        PT = sb("PT", [128, PAIRS, S])
        v = sb("v", [128, 3, PAIRS, DH])
        oT = sb("oT", [128, PAIRS, S])
        zm = sb("zm", [128, 2, E])
        zmb = sb("zmb", [128, 2, E])
        stats = sb("stats", [128, 8])
        mv = sb("mv", [128, 2])
        ve = sb("ve", [128, 2])
        rstd = sb("rstd", [128, 2])
        zn = sb("zn", [128, E])
        znT = sb("znT", [128, S])
        gl = sb("gl", [128, 3, S])
        hT = sb("hT", [128, 3, S])
        xwq = sb("xwq", [128, E])
        xwk = sb("xwk", [128, XG * XD])
        xwkr = sb("xwkr", [128, E])
        xwv = sb("xwv", [128, XG * XD])
        xwo = sb("xwo", [128, E])
        xtwc = sb("xtwc", [128, 1])
        dm = sb("dm", [32, 2, S])
        dmT = sb("dmT", [128, 2, B])
        ctT = sb("ctT", [128, B])
        ones = sb("ones", [128, 128])
        stx = sb("stx", [128, B * 6])
        mean0 = sb("mean0", [128, B])
        dif0 = sb("dif0", [128, B])
        ve0 = sb("ve0", [128, B])
        rstd0 = sb("rstd0", [128, B])
        ctxb = sb("ctxb", [128, 2, E])
        xn = sb("xn", [128, 2, E])
        td = sb("td", [128, 2, 2 * S])
        cxT = sb("cxT", [128, 2, 2 * S])
        qT = sb("qT", [128, 2, S])
        kblk = sb("kblk", [128, 2, XR * S])
        vaug = sb("vaug", [128, 2, XG, 32])
        dif = sb("dif", [128, S])
        x1cur = sb("x1cur", [128, E])
        dabs = sb("dabs", [128, S])
        mbr = sb("mbr", [128, S])
        lnt = sb("lnt", [128, S])
        bias = sb("bias", [128, 2, S])
        xmax = sb("xmax", [128, XH])
        xrs = sb("xrs", [128, XH])
        attn = sb("attn", [128, XH, XD])
        attnT = sb("attnT", [128, S])
        XP = qk
        XPT = qkT
        XO = sq[:, 0:512]

        bank = [ps(f"bank{i}") for i in range(8)]
        SC = bank[2:4]

        names = [
            "l_cst", "l_x", "l_xw", "l_dm", "l_ctx0", "l_ctx1", "l_qks", "l_wqk", "l_wv", "l_wo", "l_w1", "l_w2",
            "l_gb", "l_b2", "l_rot",
            "u_bf", "u_ones", "u_wkr", "u_rotq", "u_dmT", "u_dmc", "u_ct", "u_ctc", "u_st", "u_ag", "u_ve", "u_rstd",
            "u_negh", "u_vz", "u_v1", "u_zs",
            "x_xn", "x_td", "x_A1", "x_cxT", "x_dabs", "x_ln", "x_bias", "x_A2", "x_q", "x_kblk", "x_vaug", "x_S",
            "x_add", "x_max", "x_sub", "x_exp", "x_PT", "x_PTc", "x_O", "x_Oc", "x_OT", "x_rs", "x_attn", "x_aT",
            "x_aTc", "x_y", "x_x1", "x_store", "x_bn", "x_agg", "x_ve", "x_rstd", "z_ready",
            "p_zT", "p_qk", "p_v", "p_tr", "p_S", "p_PT", "p_AV", "p_y", "p_zsh", "p_znT", "p_gate", "p_a", "p_y2",
            "a_zs", "a_sq", "a_tr", "a_exp", "a_PT", "a_AV", "a_v", "a_zn", "a_gelu",
            "d_rot", "d_sumsq", "d_ss", "d_max", "d_sub", "d_sum", "d_rec", "d_P", "d_zm", "d_bn", "d_agg", "d_ve", "d_zn",
            "d_h", "d_out",
            "g_z", "g_add", "g_pow", "g_qk", "g_rstd", "g_zmb",
            "out_done",
        ]
        s = {n: sem(n) for n in names}

        def count(per_unit, unit, j, total=UNITS):
            if isinstance(unit, int):
                if unit < 0:
                    return 0
                if unit >= total:
                    return per_unit * total
            return unit * per_unit + j

        def wait(eng, name, value):
            if not (isinstance(value, int) and value <= 0):
                eng.wait_ge(s[name], value)

        def layer_of(unit):
            return unit // B if isinstance(unit, int) else unit >> 5

        def cols(unit):
            return bass.ds((unit & (B - 1)) * E, E)

        LOOP0, UNROLL = 8, 4
        LOOP1 = UNITS - 4

        def slots(eng, body):
            for n in range(-1, LOOP0):
                body(n, n)
            with eng.Fori(0, (LOOP1 - LOOP0) // UNROLL) as i:
                for k in range(UNROLL):
                    body(i * UNROLL + (LOOP0 + k), LOOP0 + k)
            for n in range(LOOP1, UNITS + 4):
                body(n, n)

        def part(n, lag, total=UNITS):
            u = n - lag
            return u, (not isinstance(u, int)) or 0 <= u < total

        def xslots(eng, body):
            for n in range(0, 4):
                body(n, n)
            with eng.Fori(0, (B - 4) // 2) as i:
                for k in range(2):
                    body(i * 2 + (4 + k), 4 + k)
            for n in range(B, B + 2):
                body(n, n)

        block = es.enter_context(nc.Block())

        @block.sync
        def _(sp):
            sp.dma_start(cst[:, :], consts).then_inc(s["l_cst"], 16)
            sp.dma_start(dm[:, 0, :], deltas).then_inc(s["l_dm"], 16)
            sp.dma_start(dm[:, 1, :], mask).then_inc(s["l_dm"], 16)
            xr = x.rearrange("b s e -> s b e")
            for c in range(4):
                sp.dma_start(zv[:, 8 * c:8 * c + 8, :], xr[:, 8 * c:8 * c + 8, :]).then_inc(s["l_x"], 16)
            for t, src in ((xwq[:, :], xWq), (xwk[:, :], xWk), (xwv[:, :], xWv),
                           (xtwc[:, :], xtw.partition_broadcast(128))):
                sp.dma_start(t, src).then_inc(s["l_xw"], 16)
            sp.dma_start(xwo[:, :], xWo).then_inc(s["l_xw"], 16)

            def loads(layer):
                w = Wqkv[layer, :, :]
                done = B * layer
                wait(sp, "p_qk", 4 * done)
                sp.dma_start(wqkv[:, 0:2 * INNER], w[:, 0:2 * INNER]).then_inc(s["l_wqk"], 16)
                wait(sp, "d_rot", 4 * done)
                if layer == 0:
                    sp.wait_ge(s["u_rotq"], 4)
                sp.dma_start(rot[:, :], rot_all[:, layer, :]).then_inc(s["l_rot"], 16)
                wait(sp, "p_v", 3 * done)
                sp.dma_start(wqkv[:, 2 * INNER:3 * INNER], w[:, 2 * INNER:3 * INNER]).then_inc(s["l_wv"], 16)
                wait(sp, "p_y", done)
                sp.dma_start(wo[:, :, :], Wo[layer, :, :].rearrange("(p i) n -> i p n", i=128)).then_inc(s["l_wo"], 16)
                wait(sp, "a_gelu", done)
                wait(sp, "d_h", done)
                g2 = gb[:, :]
                sp.dma_start(g2[:, 0:1], lng[layer, :].rearrange("(p o) -> p o", o=1)).then_inc(s["l_gb"], 16)
                sp.dma_start(g2[:, 1:2], lnb[layer, :].rearrange("(p o) -> p o", o=1)).then_inc(s["l_gb"], 16)
                for h in range(2):
                    for c, (o, m) in enumerate(FCH):
                        src = b1[layer, h * FF + o:h * FF + o + m].rearrange("(p o) -> p o", o=1)
                        sp.dma_start(b1c[0:m, 3 * h + c:3 * h + c + 1], src).then_inc(s["l_gb"], 16)
                wait(sp, "p_a", done)
                sp.dma_start(w1[:, :], W1[layer, :, :]).then_inc(s["l_w1"], 16)
                wait(sp, "p_y2", done)
                for c, (o, m) in enumerate(FCH):
                    sp.dma_start(w2[0:m, c, :], W2[layer, o:o + m, :]).then_inc(s["l_w2"], 16)
                wait(sp, "g_zmb", done)
                sp.dma_start(b2r[:, :], b2[layer, :].partition_broadcast(128)).then_inc(s["l_b2"], 16)

            sp.dma_start(qks[:, 0, :], qs.rearrange("l d -> (l d)").partition_broadcast(128)).then_inc(s["l_qks"], 16)
            sp.dma_start(qks[:, 1, :], ks.rearrange("l d -> (l d)").partition_broadcast(128)).then_inc(s["l_qks"], 16)

            for b in range(B):
                if b >= 2:
                    sp.wait_ge(s["x_A1"], b - 1)
                sp.dma_start(ctxb[:, b % 2, :], ctx[b, :, :]).then_inc(s[f"l_ctx{b % 2}"], 16)
                if b == 1:
                    loads(0)
            for layer in range(1, DEPTH):
                loads(layer)
            ov = out.rearrange("b s e -> s b e")
            for c in range(8):
                sp.wait_ge(s["d_out"], c + 1)
                sp.dma_start(ov[:, 4 * c:4 * c + 4, :], x1v[:, 4 * c:4 * c + 4, :]).then_inc(s["out_done"], 16)
            sp.wait_ge(s["out_done"], 128)

        @block.gpsimd
        def _(pool):
            g = nc.gpsimd
            g.memset(half_neg[:, :], -0.5).then_inc(s["u_negh"], 1)
            g.memset(ones[:, :], 1.0).then_inc(s["u_ones"], 1)
            g.memset(vaug[:, :, :, :], 0.0).then_inc(s["u_vz"], 1)
            pool.wait_ge(s["u_vz"], 1)
            g.memset(zsT[64:128, :, 0:1], 0.0).then_inc(s["u_zs"], 1)
            pool.wait_ge(s["u_zs"], 1)
            g.memset(vaug[:, :, :, XD:XD + 1], 1.0).then_inc(s["u_v1"], 1)
            pool.wait_ge(s["l_cst"], 16)
            pool.wait_ge(s["l_qks"], 32)
            for k in range(2):
                sc = qks[:, k, :].rearrange("p (l d) -> p l d", l=DEPTH)
                for c in range(2):
                    o = 128 * k + 64 * c
                    g.tensor_tensor(rot_all[:, :, o:o + 64], sc,
                                    rotc[:, o:o + 64].unsqueeze(1).to_broadcast([128, DEPTH, DH]),
                                    ALU.mult).then_inc(s["u_rotq"], 1)
            pool.wait_ge(s["u_ve"], 1)
            pool.wait_ge(s["u_negh"], 1)
            g.tensor_tensor(rstd0[:, :], ve0[:, :], half_neg[:, 0:B], ALU.pow).then_inc(s["u_rstd"], 1)
            with pool.Fori(0, B) as b:
                pool.wait_ge(s["x_ve"], b + 1)
                g.tensor_tensor(rstd[:, 0:1], ve[:, 0:1], half_neg[:, 0:1], ALU.pow).then_inc(s["x_rstd"], 1)

            def slot(n, k):
                zu, z_on = part(n, -1, UNITS + 1)
                a, a_on = part(n, 0)
                d, d_on = part(n, 4)
                pa, pd, pz = k % 2, k % 2, (k + 1) % 2
                if z_on:
                    wait(pool, "z_ready", zu + 1)
                    wait(pool, "p_zT", count(1, zu - 2, 1, UNITS + 1))
                    g.tensor_copy(zcur[:, pz, :], z_sb[:, cols(zu)]).then_inc(s["g_z"], 1)

                def add(j):
                    wait(pool, "d_rot", count(4, a, j + 1))
                    wait(pool, "p_tr", count(4, a - 2, j + 1))
                    c = slice(512 * j, 512 * j + 512)
                    o = qk[:, pa, c].rearrange("p (h c d) -> p h c d", c=2, d=32)
                    i0 = ta[:, c].rearrange("p (h c d) -> p h c d", c=2, d=32)
                    i1 = tb[:, c].rearrange("p (h c d) -> p h c d", c=2, d=32)[:, :, ::-1, :]
                    g.tensor_tensor(o, i0, i1, ALU.add).then_inc(s["g_add"], 1)

                if a_on:
                    add(0)
                if d_on:
                    wait(pool, "d_ve", count(1, d, 1))
                    g.tensor_tensor(rstd[:, pd:pd + 1], ve[:, pd:pd + 1], half_neg[:, 0:1],
                                    ALU.pow).then_inc(s["g_rstd"], 1)
                if a_on:
                    for j in range(1, 4):
                        add(j)
                if d_on:
                    wait(pool, "d_zm", count(1, d, 1))
                    wait(pool, "l_b2", 16 * layer_of(d) + 16)
                    wait(pool, "z_ready", count(1, d - 2, 1) + B if not (isinstance(d, int) and d < 2) else 0)
                    g.tensor_tensor(zmb[:, pd, :], zm[:, pd, :], b2r[:, :], ALU.add).then_inc(s["g_zmb"], 1)
                if a_on:
                    wait(pool, "d_ss", count(1, a, 1))
                    g.tensor_tensor(rn[:, pa, :], ss[:, pa, :], half_neg[:, :], ALU.pow).then_inc(s["g_pow"], 1)
                    wait(pool, "g_pow", count(1, a, 1))
                    for j in range(4):
                        wait(pool, "g_add", count(4, a, j + 1))
                        q3 = qk[:, pa, 512 * j:512 * j + 512].rearrange("p (h d) -> p h d", d=DH)
                        r3 = rn[:, pa, 8 * j:8 * j + 8].unsqueeze(2).to_broadcast([128, 8, DH])
                        g.tensor_tensor(q3, q3, r3, ALU.mult).then_inc(s["g_qk"], 1)

            slots(pool, slot)

        @block.scalar
        def _(act):
            a_ = nc.scalar
            act.preload_act_table_set("natural_log_exp_and_others")
            act.wait_ge(s["u_dmT"], 1)
            a_.activation(dmT[:, :, :].rearrange("p c b -> p (c b)"), bank[6][:, 0:64], ACT.Copy).then_inc(s["u_dmc"], 1)
            act.wait_ge(s["u_ct"], 1)
            a_.activation(ctT[:, :], bank[6][:, 64:96], ACT.Copy).then_inc(s["u_ctc"], 1)

            def xslot(n, k):
                A, A_on = part(n, 0, B)
                Bt, B_on = part(n, 1, B)
                C, C_on = part(n, 2, B)
                pA, pB = k % 2, (k - 1) % 2
                if A_on:
                    wait(act, "x_A1", count(1, A, 1, B))
                    wait(act, "x_A2", count(1, A - 2, 1, B))
                    a_.activation(cxT[:, pA, :], bank[6][:, 0:256], ACT.Copy).then_inc(s["x_cxT"], 1)
                    wait(act, "x_dabs", count(3, A, 3, B))
                    wait(act, "x_bias", count(1, A - 1, 1, B))
                    a_.activation(lnt[:, :], dabs[:, :], ACT.Ln, bias=1.0).then_inc(s["x_ln"], 1)
                if C_on:
                    for j in range(4):
                        wait(act, "x_PT", count(4, C, j + 1, B))
                        wait(act, "x_O", count(1, C - 1, 1, B))
                        a_.activation(XPT[:, 4 * j:4 * j + 4, :],
                                      bank[4 + j % 2][:, :].rearrange("p (h q) -> p h q", h=4),
                                      ACT.Copy).then_inc(s["x_PTc"], 1)
                if A_on:
                    wait(act, "x_A2", count(1, A, 1, B))
                    wait(act, "x_S", count(4, A - 2, 4, B))
                    a_.activation(qT[:, pA, :], bank[6][:, 0:128], ACT.Copy, scale=XSCALE).then_inc(s["x_q"], 1)
                if C_on:
                    wait(act, "x_O", count(1, C, 1, B))
                    wait(act, "x_OT", count(1, C - 1, 1, B))
                    a_.activation(XO, bank[7][:, :], ACT.Copy).then_inc(s["x_Oc"], 1)
                if A_on:
                    wait(act, "x_O", count(1, A - 2, 1, B))
                    wait(act, "u_v1", 1)
                    a_.activation(vaug[:, pA, :, 0:XD],
                                  bank[6][:, 256:288].rearrange("p (g d) -> p g d", g=XG),
                                  ACT.Copy).then_inc(s["x_vaug"], 1)
                if B_on:
                    for j in range(2):
                        wait(act, "x_sub", count(2, Bt, j + 1, B))
                        pr = XP[:, pB, 1024 * j:1024 * j + 1024]
                        a_.activation(pr, pr, ACT.Exp).then_inc(s["x_exp"], 1)
                if C_on:
                    wait(act, "x_aT", count(1, C, 1, B))
                    wait(act, "x_y", count(1, C - 1, 1, B))
                    a_.activation(attnT[:, :], bank[7][:, 0:128], ACT.Copy).then_inc(s["x_aTc"], 1)

            xslots(act, xslot)

            def slot(n, k):
                zu, z_on = part(n, -1, UNITS + 1)
                a, a_on = part(n, 0)
                b, b_on = part(n, 2)
                c, c_on = part(n, 3)
                d, d_on = part(n, 4)
                pb = k % 2

                def square(j):
                    wait(act, "p_qk", count(4, a, j + 1))
                    wait(act, "d_ss", count(1, a - 1, 1))
                    a_.activation(sq[:, 512 * j:512 * j + 512], bank[(k + j) % 2][:, :], ACT.Square)\
                        .then_inc(s["a_sq"], 1)

                def copy_T(j):
                    wait(act, "p_tr", count(4, b, j + 1))
                    wait(act, "p_S", count(1, b - 1, 1))
                    a_.activation(qkT[:, 4 * j:4 * j + 4, :], bank[4 + j % 2][:, :].rearrange("p (h q) -> p h q", h=4),
                                  ACT.Copy).then_inc(s["a_tr"], 1)

                if a_on:
                    square(0)
                if b_on:
                    copy_T(0)
                    copy_T(1)
                if a_on:
                    square(1)
                if b_on:
                    copy_T(2)
                    copy_T(3)
                if a_on:
                    square(2)
                    square(3)
                if c_on:
                    for j in range(3):
                        wait(act, "p_v", count(3, c, j + 1))
                        wait(act, "p_AV", count(2, c - 1, 2))
                        a_.activation(v[:, j, :, :].rearrange("p h d -> p (h d)"), bank[(k + 4 + j) % 2][:, :],
                                      ACT.Copy).then_inc(s["a_v"], 1)
                if z_on:
                    wait(act, "p_zT", count(1, zu, 1, UNITS + 1))
                    wait(act, "p_v", count(3, zu - 4, 3))
                    if isinstance(zu, int) and zu < 4:
                        wait(act, "u_zs", 1)
                    t = zsT[:, (k + 1) % 4, :]
                    a_.activation(t[0:64, :], bank[7][0:64, 0:128], ACT.Copy).then_inc(s["a_zs"], 1)
                    a_.activation(t[64:128, 1:128], bank[7][64:128, 0:127], ACT.Copy).then_inc(s["a_zs"], 1)
                if d_on:
                    wait(act, "p_znT", count(1, d, 1))
                    wait(act, "l_gb", 128 * layer_of(d) + 128)
                    wait(act, "p_a", count(1, d - 1, 1))
                    a_.activation(znT[:, :], bank[6][:, 0:128], ACT.Identity, scale=gb[:, 0:1], bias=gb[:, 1:2])\
                        .then_inc(s["a_zn"], 1)
                if c_on:
                    for j in range(2):
                        wait(act, "p_PT", count(2, c, j + 1))
                        wait(act, "p_AV", count(2, c - 1, 2))
                        a_.activation(PT[:, 4 * j:4 * j + 4, :],
                                      bank[4 + j][:, :].rearrange("p (h q) -> p h q", h=4),
                                      ACT.Copy).then_inc(s["a_PT"], 1)
                if d_on:
                    wait(act, "p_gate", count(1, d, 1))
                    wait(act, "d_h", count(1, d - 1, 1))
                    for j, (_, m) in enumerate(FCH):
                        ins = a_.activation(gl[0:m, j, :], bank[7][0:m, 128 * j:128 * j + 128], ACT.Gelu,
                                            bias=b1c[0:m, 3 + j:4 + j])
                    ins.then_inc(s["a_gelu"], 1)
                if c_on:
                    for j in range(2):
                        wait(act, "p_AV", count(2, c, j + 1))
                        wait(act, "p_y", count(1, c - 1, 1))
                        a_.activation(oT[:, 4 * j:4 * j + 4, :],
                                      bank[4 + j][:, :].rearrange("p (h q) -> p h q", h=4),
                                      ACT.Copy).then_inc(s["a_AV"], 1)
                if b_on:
                    wait(act, "d_sub", count(1, b, 1))
                    a_.activation(P[:, pb, :], P[:, pb, :], ACT.Exp).then_inc(s["a_exp"], 1)

            slots(act, slot)

        @block.vector
        def _(dve):
            v_ = nc.vector
            dve.wait_ge(s["l_cst"], 16)
            v_.tensor_copy(identb[:, :], ident).then_inc(s["u_bf"], 1)
            v_.tensor_copy(maskb[:, :], cst[:, C_MASK:C_MASK + 64]).then_inc(s["u_bf"], 1)
            dve.wait_ge(s["l_xw"], 80)
            v_.tensor_copy(xwkr[:, :].rearrange("p (g r d) -> p g r d", g=XG, r=XR),
                           xwk[:, :].rearrange("p (g d) -> p g d", g=XG).unsqueeze(2).to_broadcast([128, XG, XR, XD]))\
                .then_inc(s["u_wkr"], 1)
            dve.wait_ge(s["u_dmc"], 1)
            v_.tensor_scalar(dmT[:, 1, :], dmT[:, 1, :], -1.0, 1e9, ALU.add, ALU.mult).then_inc(s["u_dmc"], 1)
            dve.wait_ge(s["l_x"], 64)
            with dve.Fori(0, B) as b:
                v_.bn_stats(stx[:, bass.ds(b * 6, 6)], z_sb[:, bass.ds(b * E, E)]).then_inc(s["u_st"], 1)
            dve.wait_ge(s["u_st"], B)
            st = stx[:, :].rearrange("p (b c) -> p b c", c=6)
            v_.tensor_tensor(mean0[:, :], st[:, :, 1], st[:, :, 4], ALU.add).then_inc(s["u_ag"], 1)
            v_.tensor_tensor(dif0[:, :], st[:, :, 1], st[:, :, 4], ALU.subtract).then_inc(s["u_ag"], 1)
            v_.tensor_tensor(ve0[:, :], st[:, :, 2], st[:, :, 5], ALU.add).then_inc(s["u_ag"], 1)
            dve.wait_ge(s["u_ag"], 3)
            v_.tensor_scalar(mean0[:, :], mean0[:, :], 0.5, None, ALU.mult).then_inc(s["u_ag"], 1)
            v_.tensor_tensor(dif0[:, :], dif0[:, :], dif0[:, :], ALU.mult).then_inc(s["u_ag"], 1)
            v_.tensor_scalar(ve0[:, :], ve0[:, :], 1.0 / E, LN_EPS, ALU.mult, ALU.add).then_inc(s["u_ag"], 1)
            dve.wait_ge(s["u_ag"], 6)
            v_.scalar_tensor_tensor(ve0[:, :], dif0[:, :], 0.25, ve0[:, :], ALU.mult, ALU.add).then_inc(s["u_ve"], 1)
            dve.wait_ge(s["u_dmc"], 2)
            dve.wait_ge(s["u_rstd"], 1)
            dve.wait_ge(s["u_ctc"], 1)
            dmf = dmT[:, :, :].rearrange("p c b -> p (c b)")

            def xslot(n, k):
                A, A_on = part(n, 0, B)
                Bt, B_on = part(n, 1, B)
                C, C_on = part(n, 2, B)
                pA, pB, pC = k % 2, (k - 1) % 2, k % 2
                if A_on:
                    wait(dve, "x_A1", count(1, A - 2, 1, B))
                    v_.tensor_scalar(xn[:, pA, :], z_sb[:, bass.ds(A * E, E)], mean0[:, bass.ds(A, 1)],
                                     rstd0[:, bass.ds(A, 1)], ALU.subtract, ALU.mult).then_inc(s["x_xn"], 1)
                    v_.tensor_scalar(td[:, pA, 0:S], tri, dmf[:, bass.ds(A, 1)], None, ALU.mult)\
                        .then_inc(s["x_td"], 1)
                    v_.tensor_scalar(td[:, pA, S:2 * S], ident, dmf[:, bass.ds(A + B, 1)], None, ALU.mult)\
                        .then_inc(s["x_td"], 1)
                if B_on:
                    for j in range(2):
                        wait(dve, "x_S", count(4, Bt, 2 * j + 2, B))
                        wait(dve, "x_PT", count(4, Bt - 2, 4, B))
                        wait(dve, "x_bias", count(1, Bt, 1, B))
                        for i in range(2):
                            v_.tensor_tensor(
                                XP[:, pB, 1024 * j + 512 * i:1024 * j + 512 * i + 512]
                                .rearrange("p (h q) -> p h q", q=S),
                                bank[2 * j + i][:, :].rearrange("p (h q) -> p h q", q=S),
                                bias[:, pB, :].unsqueeze(1).to_broadcast([128, 4, S]), ALU.add)\
                                .then_inc(s["x_add"], 1)
                        pr = XP[:, pB, 1024 * j:1024 * j + 1024].rearrange("p (h q) -> p h q", q=S)
                        wait(dve, "x_add", count(4, Bt, 2 * j + 2, B))
                        wait(dve, "x_sub", count(2, Bt - 1, j + 1, B))
                        v_.tensor_reduce(xmax[:, 8 * j:8 * j + 8], pr, AX.X, ALU.max).then_inc(s["x_max"], 1)
                        wait(dve, "x_max", count(2, Bt, j + 1, B))
                        v_.tensor_tensor(pr, pr, xmax[:, 8 * j:8 * j + 8].unsqueeze(2).to_broadcast([128, 8, S]),
                                         ALU.subtract).then_inc(s["x_sub"], 1)
                if A_on:
                    wait(dve, "x_A1", count(1, A, 1, B))
                    wait(dve, "x_ln", count(1, A - 1, 1, B))
                    wait(dve, "x_cxT", count(1, A, 1, B))
                    wait(dve, "x_bias", count(1, A - 1, 1, B))
                    v_.tensor_copy(mbr[:, :], bank[6][:, 384:512]).then_inc(s["x_dabs"], 1)
                    v_.tensor_scalar(dif[:, :], bank[6][:, 256:384], ctT[:, bass.ds(A, 1)], None,
                                     ALU.subtract).then_inc(s["x_dabs"], 1)
                    wait(dve, "x_dabs", count(3, A, 2, B))
                    v_.scalar_tensor_tensor(dabs[:, :], dif[:, :], -1.0, dif[:, :], ALU.mult, ALU.max)\
                        .then_inc(s["x_dabs"], 1)
                if C_on:
                    wait(dve, "x_OT", count(1, C, 1, B))
                    o4 = bank[7][:, :].rearrange("p (r g d) -> p r g d", r=XR, g=XG)
                    v_.reciprocal(xrs[:, :].rearrange("p (g r) -> p r g", g=XG), o4[:, :, :, XD]).then_inc(s["x_rs"], 1)
                    wait(dve, "x_rs", count(1, C, 1, B))
                    wait(dve, "x_aT", count(1, C - 1, 1, B))
                    at = attn[:, :, :].rearrange("p (g r) d -> p r g d", g=XG)
                    rs = xrs[:, :].rearrange("p (g r) -> p r g", g=XG)
                    for r in range(XR):
                        ins = v_.tensor_tensor(at[:, r, :, :], o4[:, r, :, 0:XD],
                                               rs[:, r, :].unsqueeze(2).to_broadcast([128, XG, XD]), ALU.mult)
                    ins.then_inc(s["x_attn"], 1)
                if A_on:
                    wait(dve, "x_ln", count(1, A, 1, B))
                    wait(dve, "x_dabs", count(3, A, 3, B))
                    v_.scalar_tensor_tensor(bias[:, pA, :], lnt[:, :], xtwc[:, 0:1], mbr[:, :], ALU.mult, ALU.add)\
                        .then_inc(s["x_bias"], 1)
                    wait(dve, "x_A2", count(1, A, 1, B))
                    wait(dve, "x_vaug", count(1, A, 1, B))
                    wait(dve, "x_S", count(4, A - 2, 4, B))
                    v_.tensor_tensor(kblk[:, pA, :].rearrange("p (r t) -> p r t", r=XR),
                                     bank[6][:, 128:256].unsqueeze(1).to_broadcast([128, XR, S]),
                                     blk.unsqueeze(2).to_broadcast([128, XR, S]), ALU.mult).then_inc(s["x_kblk"], 1)
                if C_on:
                    wait(dve, "x_y", count(1, C, 1, B))
                    xc = bass.ds(C * E, E)
                    v_.tensor_tensor(x1cur[:, :], bank[7][:, 0:128], z_sb[:, xc], ALU.add).then_inc(s["x_x1"], 1)
                    wait(dve, "x_x1", count(1, C, 1, B))
                    v_.bn_stats(stats[:, 0:6], x1cur[:, :]).then_inc(s["x_bn"], 1)
                    wait(dve, "x_bn", count(1, C, 1, B))
                    v_.tensor_copy(x1_sb[:, xc], x1cur[:, :]).then_inc(s["x_store"], 1)
                    v_.bn_aggr(mv[:, :], stats[:, 0:6]).then_inc(s["x_agg"], 1)
                    wait(dve, "x_agg", count(1, C, 1, B))
                    v_.tensor_scalar(ve[:, 0:1], mv[:, 1:2], LN_EPS, None, ALU.add).then_inc(s["x_ve"], 1)
                    wait(dve, "x_rstd", count(1, C, 1, B))
                    v_.tensor_scalar(z_sb[:, xc], x1cur[:, :], mv[:, 0:1], rstd[:, 0:1], ALU.subtract, ALU.mult)\
                        .then_inc(s["z_ready"], 1)

            xslots(dve, xslot)

            def slot(n, k):
                a, a_on = part(n, 0)
                b, b_on = part(n, 2)
                c, c_on = part(n, 3)
                d, d_on = part(n, 4)
                pa, pb, pc, pd = k % 2, k % 2, (k - 3) % 2, k % 2

                def rotary(j):
                    wait(dve, "a_sq", count(4, a, j + 1))
                    wait(dve, "g_add", count(4, a - 1, j + 1))
                    if j == 0:
                        wait(dve, "l_rot", 16 * layer_of(a) + 16)
                    o = 128 * (j // 2)
                    src = bank[(k + j) % 2][:, :].rearrange("p (h d) -> p h d", d=DH)
                    for t, r in ((ta, rot[:, o:o + 64]), (tb, rot[:, o + 64:o + 128])):
                        ins = v_.tensor_tensor(t[:, 512 * j:512 * j + 512].rearrange("p (h d) -> p h d", d=DH), src,
                                               r.unsqueeze(1).to_broadcast([128, 8, DH]), ALU.mult)
                    ins.then_inc(s["d_rot"], 1)

                if d_on:
                    wait(dve, "p_y", count(1, d, 1))
                    wait(dve, "p_zsh", count(1, d - 2, 1))
                    wait(dve, "g_zmb", count(1, d - 2, 1))
                    v_.tensor_tensor(zm[:, pd, :], bank[7][:, 384:512], z_sb[:, cols(d)], ALU.add)\
                        .then_inc(s["d_zm"], 1)
                if a_on:
                    rotary(0)
                if c_on:
                    wait(dve, "a_exp", count(1, c, 1))
                    pr = P[:, pc, :].rearrange("p (h t) -> p h t", t=DH)
                    v_.tensor_reduce(rowsum[:, 0, :], pr, AX.X, ALU.add).then_inc(s["d_sum"], 1)
                    wait(dve, "d_sum", count(1, c, 1))
                    v_.reciprocal(rowsum[:, 1, :], rowsum[:, 0, :]).then_inc(s["d_rec"], 1)
                    wait(dve, "d_rec", count(1, c, 1))
                    v_.tensor_tensor(pr, pr, rowsum[:, 1, :].unsqueeze(2).to_broadcast([128, HEADS, DH]),
                                     ALU.mult).then_inc(s["d_P"], 1)
                if a_on:
                    rotary(1)
                if d_on:
                    wait(dve, "p_zsh", count(1, d, 1))
                    v_.bn_stats(stats[:, 0:6], bank[6][:, 0:128]).then_inc(s["d_bn"], 1)
                if d_on:
                    wait(dve, "d_bn", count(1, d, 1))
                    dve.nop(nofuse=True)
                    v_.bn_aggr(mv[:, :], stats[:, 0:6]).then_inc(s["d_agg"], 1)
                    wait(dve, "d_agg", count(1, d, 1))
                    v_.tensor_scalar(ve[:, pd:pd + 1], mv[:, 1:2], LN_EPS, None, ALU.add).then_inc(s["d_ve"], 1)
                if a_on:
                    rotary(2)
                if d_on:
                    wait(dve, "g_rstd", count(1, d, 1))
                    wait(dve, "p_znT", count(1, d - 1, 1))
                    v_.tensor_scalar(zn[:, :], bank[6][:, 0:128], mv[:, 0:1], rstd[:, pd:pd + 1],
                                     ALU.subtract, ALU.mult).then_inc(s["d_zn"], 1)
                if a_on:
                    rotary(3)
                    wait(dve, "g_pow", count(1, a - 2, 1))
                    v_.tensor_reduce(ss[:, pa, :], sq[:, :].rearrange("p (h d) -> p h d", d=DH), AX.X, ALU.add)\
                        .then_inc(s["d_sumsq"], 1)
                    wait(dve, "d_sumsq", count(1, a, 1))
                    v_.tensor_scalar(ss[:, pa, :], ss[:, pa, :], NORM_MIN2, None, ALU.max).then_inc(s["d_ss"], 1)
                if b_on:
                    wait(dve, "p_S", count(1, b, 1))
                    wait(dve, "p_PT", count(2, b - 2, 2))
                    for e in range(2):
                        mx = rowmax[:, 8 * e:8 * e + 8]
                        v_.tensor_reduce(mx, SC[e][:, :].rearrange("p (h t) -> p h t", t=DH), AX.X, ALU.max)\
                            .then_inc(s["d_max"], 1)
                    for e in range(2):
                        mx = rowmax[:, 8 * e:8 * e + 8]
                        wait(dve, "d_max", count(2, b, e + 1))
                        ins = v_.tensor_tensor(P[:, pb, :].rearrange("p (h e t) -> p h e t", e=2, t=DH)[:, :, e, :],
                                               SC[e][:, :].rearrange("p (h t) -> p h t", t=DH),
                                               mx.unsqueeze(2).to_broadcast([128, PAIRS, DH]), ALU.subtract)
                    ins.then_inc(s["d_sub"], 1)
                if d_on:
                    wait(dve, "p_a", count(1, d, 1))
                    wait(dve, "a_gelu", count(1, d, 1))
                    wait(dve, "p_y2", count(1, d - 1, 1))
                    for j, (_, m) in enumerate(FCH):
                        ins = v_.scalar_tensor_tensor(hT[0:m, j, :], bank[6][0:m, 128 * j:128 * j + 128],
                                                      b1c[0:m, j:j + 1], gl[0:m, j, :], ALU.add, ALU.mult)
                    ins.then_inc(s["d_h"], 1)
                    wait(dve, "p_y2", count(1, d, 1))
                    wait(dve, "g_zmb", count(1, d, 1))
                    v_.tensor_tensor(z_sb[:, cols(d)], bank[6][:, 384:512], zmb[:, pd, :], ALU.add)\
                        .then_inc(s["z_ready"], 1)

            slots(dve, slot)
            dve.wait_ge(s["z_ready"], B + UNITS)
            dve.wait_ge(s["x_store"], B)
            for c in range(8):
                cc = slice(512 * c, 512 * c + 512)
                v_.tensor_tensor(x1_sb[:, cc], x1_sb[:, cc], z_sb[:, cc], ALU.add).then_inc(s["d_out"], 1)

        @block.tensor
        def _(pe):
            t_ = nc.tensor
            pe.wait_ge(s["l_cst"], 16)
            pe.wait_ge(s["l_dm"], 32)
            t_.transpose(bank[6][:, 0:32], dm[:, 0, :], ident[0:32, 0:32])
            t_.transpose(bank[6][:, 32:64], dm[:, 1, :], ident[0:32, 0:32]).then_inc(s["u_dmT"], 1)
            pe.wait_ge(s["u_dmc"], 1)
            t_.matmul(bank[6][:, 64:96], tri, dmT[:, 0, :], start=True, stop=True).then_inc(s["u_ct"], 1)
            pe.wait_ge(s["u_ctc"], 1)
            pe.wait_ge(s["u_ones"], 1)
            pe.wait_ge(s["l_xw"], 80)
            pe.wait_ge(s["u_wkr"], 1)

            def xslot(n, k):
                A, A_on = part(n, 0, B)
                Bt, B_on = part(n, 1, B)
                C, C_on = part(n, 2, B)
                pA, pB, pC = k % 2, (k - 1) % 2, k % 2
                if A_on:
                    wait(pe, f"l_ctx{pA}", 16 * (A // 2) + 16 if isinstance(A, int) else (A >> 1) * 16 + 16)
                    wait(pe, "x_xn", count(1, A, 1, B))
                    wait(pe, "x_td", count(2, A, 2, B))
                    wait(pe, "x_kblk", count(1, A - 1, 1, B))
                    wait(pe, "x_vaug", count(1, A - 1, 1, B))
                    t_.transpose(bank[6][:, 0:128], ctxb[:, pA, :], ident)
                    t_.transpose(bank[6][:, 128:256], xn[:, pA, :], ident)
                    t_.matmul(bank[6][:, 256:512], ones[:, :], td[:, pA, :], start=True, stop=True)\
                        .then_inc(s["x_A1"], 1)
                if B_on:
                    wait(pe, "x_q", count(1, Bt, 1, B))
                    wait(pe, "x_kblk", count(1, Bt, 1, B))
                    for gr in range(XG):
                        wait(pe, "x_add", count(4, Bt - 1, gr + 1, B))
                        r = slice(32 * gr, 32 * gr + 32)
                        t_.matmul(bank[gr][:, :], qT[r, pB, :], kblk[r, pB, :], start=True, stop=True)\
                            .then_inc(s["x_S"], 1)
                if C_on:
                    for j in range(4):
                        wait(pe, "x_exp", count(2, C, j // 2 + 1, B))
                        wait(pe, "x_PTc", count(4, C, j - 1, B) if j >= 2 else count(4, C - 1, j + 3, B))
                        for h in range(4):
                            hh = 4 * j + h
                            ins = t_.transpose(bank[4 + j % 2][:, 128 * h:128 * h + 128],
                                               XP[:, pC, 128 * hh:128 * hh + 128], ident)
                        ins.then_inc(s["x_PT"], 1)
                if A_on:
                    wait(pe, "x_cxT", count(1, A, 1, B))
                    wait(pe, "x_dabs", count(3, A, 2, B))
                    t_.matmul(bank[6][:, 0:128], xwq[:, :], cxT[:, pA, S:2 * S], start=True, stop=True)
                    t_.matmul(bank[6][:, 128:256], xwkr[:, :], cxT[:, pA, 0:S], start=True, stop=True)
                    t_.matmul(bank[6][:, 256:288], cxT[:, pA, 0:S], xwv[:, :], start=True, stop=True)\
                        .then_inc(s["x_A2"], 1)
                if C_on:
                    wait(pe, "x_PTc", count(4, C, 4, B))
                    wait(pe, "x_vaug", count(1, C, 1, B))
                    wait(pe, "x_x1", count(1, C - 1, 1, B))
                    for gr in range(XG):
                        ins = t_.matmul(bank[7][32 * gr:32 * gr + 32, :], vaug[:, pC, gr, :],
                                        XPT[:, 4 * gr:4 * gr + 4, :], start=True, stop=True)
                    ins.then_inc(s["x_O"], 1)
                    wait(pe, "x_Oc", count(1, C, 1, B))
                    for r in range(XR):
                        ins = t_.transpose(bank[7][:, 128 * r:128 * r + 128], XO[:, 128 * r:128 * r + 128], ident)
                    ins.then_inc(s["x_OT"], 1)
                    wait(pe, "x_attn", count(1, C, 1, B))
                    t_.transpose(bank[7][:, 0:128], attn[:, :, :].rearrange("p h d -> p (h d)"), ident)\
                        .then_inc(s["x_aT"], 1)
                    wait(pe, "x_aTc", count(1, C, 1, B))
                    t_.matmul(bank[7][:, 0:128], attnT[:, :], xwo[:, :], start=True, stop=True)\
                        .then_inc(s["x_y"], 1)

            xslots(pe, xslot)
            pe.wait_ge(s["u_bf"], 2)
            pe.wait_ge(s["x_x1"], B)

            def slot(n, k):
                zu, z_on = part(n, -1, UNITS + 1)
                a, a_on = part(n, 0)
                b, b_on = part(n, 2)
                c, c_on = part(n, 3)
                d, d_on = part(n, 4)
                pa, pb, pc, pd = k % 2, k % 2, (k - 3) % 2, k % 2

                def proj_qk(j):
                    if j == 0:
                        wait(pe, "a_zs", count(2, a, 2, UNITS + 1))
                        wait(pe, "l_wqk", 16 * layer_of(a) + 16)
                        wait(pe, "d_rot", count(4, a - 1, 4))
                        wait(pe, "a_v", count(3, c - 1, 2))
                    elif j == 1:
                        wait(pe, "a_v", count(3, c - 1, 3))
                    else:
                        wait(pe, "d_rot", count(4, a, j - 1))
                    t_.matmul(bank[(k + j) % 2][:, :], zsT[:, k % 4, :], wqkv[:, 512 * j:512 * j + 512],
                              start=True, stop=True).then_inc(s["p_qk"], 1)

                def transpose_qk(j):
                    wait(pe, "g_qk", count(4, b, j + 1))
                    if j < 2:
                        wait(pe, "a_tr", count(4, b - 1, 4))
                        wait(pe, "a_AV", count(2, c - 1, 2))
                    else:
                        wait(pe, "a_tr", count(4, b, j - 1))
                    for p in range(4):
                        ins = t_.transpose(bank[4 + j % 2][:, 128 * p:128 * p + 128],
                                           qk[:, pb, 512 * j + 128 * p:512 * j + 128 * p + 128], ident)
                    ins.then_inc(s["p_tr"], 1)

                if a_on:
                    proj_qk(0)
                if b_on:
                    transpose_qk(0)
                    transpose_qk(1)
                if a_on:
                    proj_qk(1)
                if b_on:
                    transpose_qk(2)
                    transpose_qk(3)
                if d_on:
                    wait(pe, "d_zm", count(1, d, 1))
                    wait(pe, "z_ready", (count(1, d - 1, 1) if isinstance(d, int) else d) + B)
                    t_.matmul(bank[6][:, 0:64], ident, zm[:, pd, 0:64], start=True, stop=True)
                    t_.matmul(bank[6][:, 64:128], shift, zm[:, pd, 64:128], start=True, stop=True)\
                        .then_inc(s["p_zsh"], 1)
                if a_on:
                    proj_qk(2)
                if b_on:
                    wait(pe, "a_tr", count(4, b, 4))
                    wait(pe, "d_sub", count(1, b - 1, 1))
                    for e in range(2):
                        t_.matmul(SC[e][:, :], identb[:, :], maskb[:, :].unsqueeze(1).to_broadcast([128, PAIRS, DH]),
                                  start=True, stop=False, skip_group_check=True)
                    for p in range(PAIRS):
                        for w in range(NW):
                            k0 = WIN * max(0, w - 1)
                            for e in range(2):
                                r = slice(64 * e, 64 * e + 64)
                                ins = t_.matmul(SC[e][WIN * w:WIN * w + WIN, 64 * p:64 * p + 64],
                                                qkT[r, p, WIN * w:WIN * w + WIN], qkT[r, PAIRS + p, k0:k0 + 64],
                                                start=False, stop=p == PAIRS - 1, skip_group_check=True)
                    ins.then_inc(s["p_S"], 1)
                if a_on:
                    proj_qk(3)
                if c_on:
                    wait(pe, "l_wv", 16 * layer_of(c) + 16)
                    for j in range(3):
                        if j < 2:
                            wait(pe, "d_rot", count(4, a, j + 3))
                            wait(pe, "a_v", count(3, c - 1, 3))
                        else:
                            wait(pe, "a_v", count(3, c, 1))
                        wv = wqkv[:, 2 * INNER:].rearrange("i (p e d) -> i p e d", e=2, d=DH)
                        for e in range(2):
                            ins = t_.matmul(bank[(k + 4 + j) % 2][64 * e:64 * e + 64, :],
                                            zsT[:, (k + 1) % 4, WIN * j:WIN * j + 64], wv[:, :, e, :],
                                            start=True, stop=True)
                        ins.then_inc(s["p_v"], 1)
                if z_on:
                    wait(pe, "g_z", count(1, zu, 1, UNITS + 1))
                    wait(pe, "d_zm", count(1, d, 1))
                    wait(pe, "a_zs", count(2, zu - 1, 2, UNITS + 1))
                    t_.transpose(bank[7][:, 0:128], zcur[:, (k + 1) % 2, :], ident).then_inc(s["p_zT"], 1)
                if d_on:
                    wait(pe, "d_zn", count(1, d, 1))
                    t_.transpose(bank[6][:, 0:128], zn[:, :], ident).then_inc(s["p_znT"], 1)
                if c_on:
                    for j in range(2):
                        wait(pe, "d_P", count(1, c, 1))
                        wait(pe, "a_tr", count(4, b, 3 + j))
                        wait(pe, "a_AV", count(2, c - 1, 2))
                        for p in range(4):
                            hp = 4 * j + p
                            ins = t_.transpose(bank[4 + j][:, 128 * p:128 * p + 128],
                                               P[:, pc, 128 * hp:128 * hp + 128], ident)
                        ins.then_inc(s["p_PT"], 1)
                if d_on:
                    wait(pe, "a_zn", count(1, d, 1))
                    wait(pe, "l_w1", 16 * layer_of(d) + 16)
                    wait(pe, "a_zs", count(2, zu, 2, UNITS + 1))
                    for j, (o, m) in enumerate(FCH):
                        ins = t_.matmul(bank[7][0:m, 128 * j:128 * j + 128], w1[:, FF + o:FF + o + m], znT[:, :],
                                        start=True, stop=True)
                    ins.then_inc(s["p_gate"], 1)
                    for j, (o, m) in enumerate(FCH):
                        ins = t_.matmul(bank[6][0:m, 128 * j:128 * j + 128], w1[:, o:o + m], znT[:, :],
                                        start=True, stop=True)
                    ins.then_inc(s["p_a"], 1)
                if c_on:
                    for j in range(2):
                        wait(pe, "a_PT", count(2, c, j + 1))
                        if j == 0:
                            wait(pe, "a_v", count(3, c, 3))
                        pe.nop(nofuse=True)
                        for p in range(4):
                            hp = 4 * j + p
                            for st, q0, nq in ((0, 0, 64), (1, 64, 32), (2, 96, 32)):
                                for e in range(2):
                                    r = slice(64 * e, 64 * e + 64)
                                    ins = t_.matmul(bank[4 + j][r, 128 * p + q0:128 * p + q0 + nq], v[r, st, hp, :],
                                                    PT[r, hp, q0:q0 + nq], start=True, stop=True)
                        ins.then_inc(s["p_AV"], 1)
                if d_on:
                    wait(pe, "d_h", count(1, d, 1))
                    wait(pe, "l_w2", 48 * layer_of(d) + 48)
                    for j, (_, m) in enumerate(FCH):
                        ins = t_.matmul(bank[6][:, 384:512], hT[0:m, j, :], w2[0:m, j, :], start=j == 0, stop=j == 2)
                    ins.then_inc(s["p_y2"], 1)
                if c_on:
                    wait(pe, "a_AV", count(2, c, 2))
                    wait(pe, "l_wo", 16 * layer_of(c) + 16)
                    wait(pe, "a_gelu", count(1, d, 1))
                    wait(pe, "a_zs", count(2, zu, 2, UNITS + 1))
                    for p in range(PAIRS):
                        ins = t_.matmul(bank[7][:, 384:512], oT[:, p, :], wo[:, p, :], start=p == 0,
                                        stop=p == PAIRS - 1)
                    ins.then_inc(s["p_y"], 1)

            slots(pe, slot)


_INS = ['x', 'ctx_1024', 'fside_BxS2_0', 'mask_BxS2_ff1', 'L0_xattn_Wq', 'L0_xattn_Wk', 'L0_xattn_Wv', 'L0_xattn_Wo',
        'L0_xattn_time_bias_weight', 'L0_ffn_Wqkv', 'L0_ffn_q_scale', 'L0_ffn_k_scale', 'L0_ffn_Wo', 'L0_ffn_ln_g',
        'L0_ffn_ln_b', 'L0_ffn_W1', 'L0_ffn_b1', 'L0_ffn_W2', 'L0_ffn_b2']


def kernel(**inputs):
    import concourse.bacc as bacc
    from concourse.bass_utils import run_bass_kernel_spmd

    nc = bacc.Bacc("TRN2", target_bir_lowering=False, num_devices=1)
    arrays, args = {}, []
    for name in _INS:
        a = np.ascontiguousarray(inputs[name])
        if a.ndim == 0 or name == 'L0_xattn_time_bias_weight':
            a = a.reshape(1)
        arrays[name] = a
    arrays["consts"] = constants()
    for name, a in arrays.items():
        args.append(nc.dram_tensor(name, a.shape, mybir.dt.from_np(a.dtype), kind="ExternalInput").ap())
    args.append(nc.dram_tensor("out", (B, S, E), F32, kind="ExternalOutput").ap())
    build(nc, *args)
    r = run_bass_kernel_spmd(nc, [arrays], core_ids=[0])
    return r.results[0]["out"]
```

```python
from contextlib import ExitStack

import numpy as np

import concourse.bass as bass
from concourse import mybir

F32 = mybir.dt.float32
BF16 = mybir.dt.bfloat16
ALU = mybir.AluOpType
ACT = mybir.ActivationFunctionType
AX = mybir.AxisListType

B, S, E = 32, 128, 128
XH, XG, XD = 16, 4, 8
XR = XH // XG
XSCALE = 1.0 / float(XD) ** 0.5
DEPTH, HEADS, DH, WIN = 6, 16, 64, 32
INNER = HEADS * DH
PAIRS = HEADS // 2
NW = S // WIN
FF = int(E * 4 * 2 / 3)
FCH = [(0, 128), (128, 128), (256, FF - 256)]
QK_SCALE = 8.0
UNITS = DEPTH * B
LN_EPS = 1e-5
NORM_MIN2 = 1e-24
MASKED = -(2.0 ** 120)

C_ID, C_SH, C_TRI, C_ROT, C_MASK, C_BLK, C_END = 0, 128, 256, 384, 640, 704, 708


def constants():
    c = np.zeros((128, C_END), np.float32)
    r = np.arange(128)
    c[:, C_ID:C_ID + 128] = np.eye(128)
    c[r[:-1], C_SH + 1 + r[:-1]] = 1.0
    c[:, C_TRI:C_TRI + 128] = r[:, None] <= r[None, :]
    half = np.arange(0, DH, 2, dtype=np.float32)
    inv = (1.0 / np.float32(10000.0) ** (half / np.float32(DH))).astype(np.float32)
    t = np.arange(S, dtype=np.float32)
    f = (t[:, None] * inv[None, :]).astype(np.float32)
    base = (half + np.float32(0.4 * DH)) / np.float32(1.4 * DH)
    scale = (base[None, :] ** ((t - S // 2) / (WIN // 2))[:, None]).astype(np.float32)
    cos, sin = np.cos(f).astype(np.float32), np.sin(f).astype(np.float32)
    for k, s in enumerate((scale * np.float32(QK_SCALE), np.float32(1.0) / scale)):
        o = C_ROT + 128 * k
        c[:, o:o + 64] = np.concatenate([cos * s, cos * s], 1)
        c[:, o + 64:o + 128] = np.concatenate([sin * s, -(sin * s)], 1)
    w = r // WIN
    key = np.where(w == 0, 0, (w - 1) * WIN)[:, None] + np.arange(64)[None, :]
    ok = (key <= r[:, None]) & (key + WIN >= r[:, None])
    c[:, C_MASK:C_MASK + 64] = np.where(ok, 0.0, MASKED)
    c[:, C_BLK:C_BLK + XR] = (r[:, None] // XD) % XR == np.arange(XR)[None, :]
    return c


def build(nc, x, ctx, deltas, mask, xWq, xWk, xWv, xWo, xtw, Wqkv, qs, ks, Wo, lng, lnb, W1, b1, W2, b2, consts, out):
    es = ExitStack()
    with es:
        def sb(name, shape, dt=F32):
            return es.enter_context(nc.sbuf_tensor(name, shape, dt))

        def ps(name):
            return es.enter_context(nc.psum_tensor(name, [128, 512], F32))

        def sem(name):
            return es.enter_context(nc.semaphore(name))

        cst = sb("cst", [128, C_END])
        ident = cst[:, C_ID:C_ID + 128]
        shift = cst[:, C_SH:C_SH + 128]
        tri = cst[:, C_TRI:C_TRI + 128]
        rotc = cst[:, C_ROT:C_ROT + 256]
        blk = cst[:, C_BLK:C_BLK + XR]
        identb = sb("identb", [128, 128], BF16)
        maskb = sb("maskb", [128, 64], BF16)
        z_sb = sb("z_sb", [128, B * E])
        x1_sb = sb("x1_sb", [128, B * E])
        zv = z_sb[:, :].rearrange("p (b e) -> p b e", b=B)
        x1v = x1_sb[:, :].rearrange("p (b e) -> p b e", b=B)
        wqkv = sb("wqkv", [128, 3 * INNER])
        wo = sb("wo", [128, PAIRS, E])
        w1 = sb("w1", [128, 2 * FF])
        w2 = sb("w2", [128, 3, E])
        gb = sb("gb", [128, 2])
        b1c = sb("b1c", [128, 6])
        b2r = sb("b2r", [128, E])
        rot = sb("rot", [128, 4 * DH])
        rot_all = sb("rot_all", [128, DEPTH, 4 * DH])
        qks = sb("qks", [128, 2, DEPTH * DH])
        zcur = sb("zcur", [128, 2, E])
        zsT = sb("zsT", [128, 4, S])
        sq = sb("sq", [128, 2 * INNER])
        ta = sb("ta", [128, 2 * INNER])
        tb = sb("tb", [128, 2 * INNER])
        qk = sb("qk", [128, 2, 2 * INNER])
        ss = sb("ss", [128, 2, 2 * HEADS])
        rn = sb("rn", [128, 2, 2 * HEADS])
        half_neg = sb("half_neg", [128, 2 * HEADS])
        qkT = sb("qkT", [128, 2 * PAIRS, S])
        P = sb("P", [128, 2, HEADS * DH])
        rowmax = sb("rowmax", [128, HEADS])
        rowsum = sb("rowsum", [128, 2, HEADS])
        PT = sb("PT", [128, PAIRS, S])
        vt = sb("vt", [128, 2, 2, INNER // 2])
        vs = sb("vs", [128, 2, 2, INNER // 2])
        oT = sb("oT", [128, PAIRS, S])
        zm = sb("zm", [128, 2, E])
        zmb = sb("zmb", [128, 2, E])
        stats = sb("stats", [128, 8])
        mv = sb("mv", [128, 2])
        ve = sb("ve", [128, 2])
        rstd = sb("rstd", [128, 2])
        zn = sb("zn", [128, E])
        znT = sb("znT", [128, S])
        gl = sb("gl", [128, 3, S])
        hT = sb("hT", [128, 3, S])
        xwq = sb("xwq", [128, E])
        xwk = sb("xwk", [128, XG * XD])
        xwkr = sb("xwkr", [128, E])
        xwv = sb("xwv", [128, XG * XD])
        xwo = sb("xwo", [128, E])
        xtwc = sb("xtwc", [128, 1])
        dm = sb("dm", [32, 2, S])
        dmT = sb("dmT", [128, 2, B])
        ctT = sb("ctT", [128, B])
        ones = sb("ones", [128, 128])
        stx = sb("stx", [128, B * 6])
        mean0 = sb("mean0", [128, B])
        dif0 = sb("dif0", [128, B])
        ve0 = sb("ve0", [128, B])
        rstd0 = sb("rstd0", [128, B])
        ctxb = sb("ctxb", [128, 2, E])
        xn = sb("xn", [128, 2, E])
        td = sb("td", [128, 2, 2 * S])
        cxT = sb("cxT", [128, 2, 2 * S])
        qT = sb("qT", [128, 2, S])
        kblk = sb("kblk", [128, 2, XR * S])
        vaug = sb("vaug", [128, 2, XG, 32])
        dif = sb("dif", [128, S])
        x1cur = sb("x1cur", [128, E])
        dabs = sb("dabs", [128, S])
        mbr = sb("mbr", [128, S])
        lnt = sb("lnt", [128, S])
        bias = sb("bias", [128, 2, S])
        xmax = sb("xmax", [128, XH])
        xrs = sb("xrs", [128, XH])
        attn = sb("attn", [128, XH, XD])
        attnT = sb("attnT", [128, S])
        XP = qk
        XPT = qkT
        XO = sq[:, 0:512]

        bank = [ps(f"bank{i}") for i in range(8)]
        SC = bank[2:4]

        names = [
            "l_cst", "l_x", "l_xw", "l_dm", "l_ctx0", "l_ctx1", "l_qks", "l_wqk", "l_wv", "l_wo", "l_w1", "l_w2",
            "l_gb", "l_b2", "l_rot", "l_v0", "l_v1",
            "u_bf", "u_ones", "u_wkr", "u_rotq", "u_dmT", "u_dmc", "u_ct", "u_ctc", "u_st", "u_ag", "u_ve", "u_rstd",
            "u_negh", "u_vz", "u_v1", "u_zs",
            "x_xn", "x_td", "x_A1", "x_cxT", "x_dabs", "x_ln", "x_bias", "x_A2", "x_q", "x_kblk", "x_vaug", "x_S",
            "x_add", "x_max", "x_sub", "x_exp", "x_PT", "x_PTc", "x_O", "x_Oc", "x_OT", "x_rs", "x_attn", "x_aT",
            "x_aTc", "x_y", "x_x1", "x_store", "x_bn", "x_agg", "x_ve", "x_rstd", "z_ready",
            "p_zT", "p_qk", "p_v", "p_tr", "p_S", "p_PT", "p_AV", "p_y", "p_zsh", "p_znT", "p_gate", "p_a", "p_y2",
            "a_zs", "a_sq", "a_tr", "a_exp", "a_PT", "a_AV", "a_v", "a_zn", "a_gelu",
            "d_rot", "d_sumsq", "d_ss", "d_max", "d_sub", "d_sum", "d_rec", "d_P", "d_zm", "d_bn", "d_agg", "d_ve", "d_zn",
            "d_h", "d_out",
            "g_z", "g_add", "g_pow", "g_qk", "g_rstd", "g_zmb",
            "out_done",
        ]
        s = {n: sem(n) for n in names}

        def count(per_unit, unit, j, total=UNITS):
            if isinstance(unit, int):
                if unit < 0:
                    return 0
                if unit >= total:
                    return per_unit * total
            return unit * per_unit + j

        def wait(eng, name, value):
            if not (isinstance(value, int) and value <= 0):
                eng.wait_ge(s[name], value)

        def layer_of(unit):
            return unit // B if isinstance(unit, int) else unit >> 5

        def cols(unit):
            return bass.ds((unit & (B - 1)) * E, E)

        LOOP0, UNROLL = 8, 4
        LOOP1 = UNITS - 4

        def slots(eng, body):
            for n in range(-1, LOOP0):
                body(n, n)
            with eng.Fori(0, (LOOP1 - LOOP0) // UNROLL) as i:
                for k in range(UNROLL):
                    body(i * UNROLL + (LOOP0 + k), LOOP0 + k)
            for n in range(LOOP1, UNITS + 4):
                body(n, n)

        def part(n, lag, total=UNITS):
            u = n - lag
            return u, (not isinstance(u, int)) or 0 <= u < total

        def xslots(eng, body):
            for n in range(0, 4):
                body(n, n)
            with eng.Fori(0, (B - 6) // 2) as i:
                for k in range(2):
                    body(i * 2 + (4 + k), 4 + k)
            for n in range(B - 2, B + 3):
                body(n, n)

        block = es.enter_context(nc.Block())

        @block.sync
        def _(sp):
            sp.dma_start(cst[:, :], consts).then_inc(s["l_cst"], 16)
            sp.dma_start(dm[:, 0, :], deltas).then_inc(s["l_dm"], 16)
            sp.dma_start(dm[:, 1, :], mask).then_inc(s["l_dm"], 16)
            xr = x.rearrange("b s e -> s b e")
            for c in range(4):
                sp.dma_start(zv[:, 8 * c:8 * c + 8, :], xr[:, 8 * c:8 * c + 8, :]).then_inc(s["l_x"], 16)
            for t, src in ((xwq[:, :], xWq), (xwk[:, :], xWk), (xwv[:, :], xWv),
                           (xtwc[:, :], xtw.partition_broadcast(128))):
                sp.dma_start(t, src).then_inc(s["l_xw"], 16)
            sp.dma_start(xwo[:, :], xWo).then_inc(s["l_xw"], 16)

            def load_qk(layer):
                w = Wqkv[layer, :, :]
                wait(sp, "p_qk", 4 * B * layer)
                sp.dma_start(wqkv[:, 0:2 * INNER], w[:, 0:2 * INNER]).then_inc(s["l_wqk"], 16)
                wait(sp, "d_rot", 4 * B * layer)
                if layer == 0:
                    sp.wait_ge(s["u_rotq"], 4)
                sp.dma_start(rot[:, :], rot_all[:, layer, :]).then_inc(s["l_rot"], 16)

            def load_v(layer):
                w = Wqkv[layer, :, :]
                wait(sp, "p_v", 2 * B * layer)
                sp.dma_start(wqkv[:, 2 * INNER:3 * INNER], w[:, 2 * INNER:3 * INNER]).then_inc(s["l_wv"], 16)

            def load_o(layer):
                wait(sp, "p_y", B * layer)
                sp.dma_start(wo[:, :, :], Wo[layer, :, :].rearrange("(p i) n -> i p n", i=128)).then_inc(s["l_wo"], 16)

            def load_ffn(layer):
                done = B * layer
                wait(sp, "a_gelu", done)
                wait(sp, "d_h", done)
                for o, src in ((0, lng), (1, lnb)):
                    sp.dma_start(gb[:, o:o + 1], src[layer, :].rearrange("(p o) -> p o", o=1)).then_inc(s["l_gb"], 16)
                for h in range(2):
                    for c, (o, m) in enumerate(FCH):
                        src = b1[layer, h * FF + o:h * FF + o + m].rearrange("(p o) -> p o", o=1)
                        sp.dma_start(b1c[0:m, 3 * h + c:3 * h + c + 1], src).then_inc(s["l_gb"], 16)
                wait(sp, "p_a", done)
                sp.dma_start(w1[:, :], W1[layer, :, :]).then_inc(s["l_w1"], 16)
                wait(sp, "p_y2", done)
                for c, (o, m) in enumerate(FCH):
                    sp.dma_start(w2[0:m, c, :], W2[layer, o:o + m, :]).then_inc(s["l_w2"], 16)
                wait(sp, "g_zmb", done)
                sp.dma_start(b2r[:, :], b2[layer, :].partition_broadcast(128)).then_inc(s["l_b2"], 16)

            def shift_v(u, par):
                for e in range(2):
                    wait(sp, "a_v", count(2, u, e + 1))
                    wait(sp, "p_AV", count(2, u - 2, 2))
                    r = slice(64 * e, 64 * e + 64)
                    for j, t0 in enumerate((32, 64 - 64 * e)):
                        sp.dma_start(vs[r, par, j, :], vt[t0:t0 + 64, par, e, :]).then_inc(s[f"l_v{par}"], 16)

            sp.dma_start(qks[:, 0, :], qs.rearrange("l d -> (l d)").partition_broadcast(128)).then_inc(s["l_qks"], 16)
            sp.dma_start(qks[:, 1, :], ks.rearrange("l d -> (l d)").partition_broadcast(128)).then_inc(s["l_qks"], 16)

            for b in range(B):
                if b >= 2:
                    sp.wait_ge(s["x_A1"], b - 1)
                sp.dma_start(ctxb[:, b % 2, :], ctx[b, :, :]).then_inc(s[f"l_ctx{b % 2}"], 16)
                if b == 1:
                    load_qk(0)
                    load_v(0)
                    load_o(0)
                    load_ffn(0)
            for layer in range(DEPTH):
                first = B * layer + 2
                if layer == 0:
                    shift_v(0, 0)
                    shift_v(1, 1)
                with sp.Fori(0, (B - 6) // 2) as i:
                    for k in range(2):
                        shift_v(i * 2 + (first + k), k)
                shift_v(B * layer + B - 4, 0)
                if layer + 1 < DEPTH:
                    load_qk(layer + 1)
                for k in range(3):
                    shift_v(B * layer + B - 3 + k, (1 + k) % 2)
                if layer + 1 < DEPTH:
                    load_v(layer + 1)
                    shift_v(B * layer + B, 0)
                    load_o(layer + 1)
                    shift_v(B * layer + B + 1, 1)
                    load_ffn(layer + 1)
            ov = out.rearrange("b s e -> s b e")
            for c in range(8):
                sp.wait_ge(s["d_out"], c + 1)
                sp.dma_start(ov[:, 4 * c:4 * c + 4, :], x1v[:, 4 * c:4 * c + 4, :]).then_inc(s["out_done"], 16)
            sp.wait_ge(s["out_done"], 128)

        @block.gpsimd
        def _(pool):
            g = nc.gpsimd
            g.memset(half_neg[:, :], -0.5).then_inc(s["u_negh"], 1)
            g.memset(ones[:, :], 1.0).then_inc(s["u_ones"], 1)
            g.memset(vaug[:, :, :, :], 0.0).then_inc(s["u_vz"], 1)
            pool.wait_ge(s["u_vz"], 1)
            g.memset(zsT[64:128, :, 0:1], 0.0).then_inc(s["u_zs"], 1)
            pool.wait_ge(s["u_zs"], 1)
            g.memset(vaug[:, :, :, XD:XD + 1], 1.0).then_inc(s["u_v1"], 1)
            pool.wait_ge(s["l_cst"], 16)
            pool.wait_ge(s["l_qks"], 32)
            for k in range(2):
                sc = qks[:, k, :].rearrange("p (l d) -> p l d", l=DEPTH)
                for c in range(2):
                    o = 128 * k + 64 * c
                    g.tensor_tensor(rot_all[:, :, o:o + 64], sc,
                                    rotc[:, o:o + 64].unsqueeze(1).to_broadcast([128, DEPTH, DH]),
                                    ALU.mult).then_inc(s["u_rotq"], 1)
            pool.wait_ge(s["u_ve"], 1)
            pool.wait_ge(s["u_negh"], 1)
            g.tensor_tensor(rstd0[:, :], ve0[:, :], half_neg[:, 0:B], ALU.pow).then_inc(s["u_rstd"], 1)

            def xslot(n, k):
                Bt, B_on = part(n, 1, B)
                D, D_on = part(n, 3, B)
                pB = (k - 1) % 2
                if B_on:
                    for j in range(2):
                        wait(pool, "x_max", count(2, Bt, j + 1, B))
                        for i in range(2):
                            hh = 8 * j + 4 * i
                            pr = XP[:, pB, 128 * hh:128 * hh + 512].rearrange("p (h q) -> p h q", q=S)
                            g.tensor_tensor(pr, pr, xmax[:, hh:hh + 4].unsqueeze(2).to_broadcast([128, 4, S]),
                                            ALU.subtract).then_inc(s["x_sub"], 1)
                if D_on:
                    wait(pool, "x_ve", count(1, D, 1, B))
                    g.tensor_tensor(rstd[:, 0:1], ve[:, 0:1], half_neg[:, 0:1], ALU.pow).then_inc(s["x_rstd"], 1)

            xslots(pool, xslot)

            def slot(n, k):
                zu, z_on = part(n, -1, UNITS + 1)
                a, a_on = part(n, 0)
                d, d_on = part(n, 4)
                pa, pd, pz = k % 2, k % 2, (k + 1) % 2
                if z_on:
                    wait(pool, "z_ready", zu + 1)
                    wait(pool, "p_zT", count(1, zu - 2, 1, UNITS + 1))
                    g.tensor_copy(zcur[:, pz, :], z_sb[:, cols(zu)]).then_inc(s["g_z"], 1)

                def add(j):
                    wait(pool, "d_rot", count(4, a, j + 1))
                    wait(pool, "p_tr", count(4, a - 2, j + 1))
                    c = slice(512 * j, 512 * j + 512)
                    o = qk[:, pa, c].rearrange("p (h c d) -> p h c d", c=2, d=32)
                    i0 = ta[:, c].rearrange("p (h c d) -> p h c d", c=2, d=32)
                    i1 = tb[:, c].rearrange("p (h c d) -> p h c d", c=2, d=32)[:, :, ::-1, :]
                    g.tensor_tensor(o, i0, i1, ALU.add).then_inc(s["g_add"], 1)

                if a_on:
                    add(0)
                if d_on:
                    wait(pool, "d_ve", count(1, d, 1))
                    g.tensor_tensor(rstd[:, pd:pd + 1], ve[:, pd:pd + 1], half_neg[:, 0:1],
                                    ALU.pow).then_inc(s["g_rstd"], 1)
                if a_on:
                    for j in range(1, 4):
                        add(j)
                if d_on:
                    wait(pool, "d_zm", count(1, d, 1))
                    wait(pool, "l_b2", 16 * layer_of(d) + 16)
                    wait(pool, "z_ready", count(1, d - 2, 1) + B if not (isinstance(d, int) and d < 2) else 0)
                    g.tensor_tensor(zmb[:, pd, :], zm[:, pd, :], b2r[:, :], ALU.add).then_inc(s["g_zmb"], 1)
                if a_on:
                    wait(pool, "d_ss", count(1, a, 1))
                    g.tensor_tensor(rn[:, pa, :], ss[:, pa, :], half_neg[:, :], ALU.pow).then_inc(s["g_pow"], 1)
                    wait(pool, "g_pow", count(1, a, 1))
                    for j in range(4):
                        wait(pool, "g_add", count(4, a, j + 1))
                        q3 = qk[:, pa, 512 * j:512 * j + 512].rearrange("p (h d) -> p h d", d=DH)
                        r3 = rn[:, pa, 8 * j:8 * j + 8].unsqueeze(2).to_broadcast([128, 8, DH])
                        g.tensor_tensor(q3, q3, r3, ALU.mult).then_inc(s["g_qk"], 1)

            slots(pool, slot)

        @block.scalar
        def _(act):
            a_ = nc.scalar
            act.preload_act_table_set("natural_log_exp_and_others")
            act.wait_ge(s["u_dmT"], 1)
            a_.activation(dmT[:, :, :].rearrange("p c b -> p (c b)"), bank[6][:, 0:64], ACT.Copy).then_inc(s["u_dmc"], 1)
            act.wait_ge(s["u_ct"], 1)
            a_.activation(ctT[:, :], bank[6][:, 64:96], ACT.Copy).then_inc(s["u_ctc"], 1)

            def xslot(n, k):
                A, A_on = part(n, 0, B)
                Bt, B_on = part(n, 1, B)
                C, C_on = part(n, 2, B)
                D, D_on = part(n, 3, B)
                pA, pB = k % 2, (k - 1) % 2
                if A_on:
                    wait(act, "x_A1", count(1, A, 1, B))
                    wait(act, "x_A2", count(1, A - 2, 1, B))
                    a_.activation(cxT[:, pA, :], bank[6][:, 0:256], ACT.Copy).then_inc(s["x_cxT"], 1)
                if D_on:
                    wait(act, "x_aT", count(1, D, 1, B))
                    wait(act, "x_y", count(1, D - 1, 1, B))
                    a_.activation(attnT[:, :], bank[7][:, 0:128], ACT.Copy).then_inc(s["x_aTc"], 1)
                if C_on:
                    for j in range(4):
                        wait(act, "x_PT", count(4, C, j + 1, B))
                        wait(act, "x_O", count(1, C - 1, 1, B))
                        a_.activation(XPT[:, 4 * j:4 * j + 4, :],
                                      bank[4 + j % 2][:, :].rearrange("p (h q) -> p h q", h=4),
                                      ACT.Copy).then_inc(s["x_PTc"], 1)
                if A_on:
                    wait(act, "x_dabs", count(3, A, 3, B))
                    wait(act, "x_bias", count(1, A - 1, 1, B))
                    a_.activation(lnt[:, :], dabs[:, :], ACT.Ln, bias=1.0).then_inc(s["x_ln"], 1)
                    wait(act, "x_A2", count(1, A, 1, B))
                    wait(act, "x_S", count(4, A - 2, 4, B))
                    a_.activation(qT[:, pA, :], bank[6][:, 0:128], ACT.Copy, scale=XSCALE).then_inc(s["x_q"], 1)
                    wait(act, "x_O", count(1, A - 2, 1, B))
                    wait(act, "u_v1", 1)
                    a_.activation(vaug[:, pA, :, 0:XD],
                                  bank[6][:, 256:288].rearrange("p (g d) -> p g d", g=XG),
                                  ACT.Copy).then_inc(s["x_vaug"], 1)
                for j in range(2):
                    if B_on:
                        wait(act, "x_sub", count(4, Bt, 2 * j + 2, B))
                        pr = XP[:, pB, 1024 * j:1024 * j + 1024]
                        a_.activation(pr, pr, ACT.Exp).then_inc(s["x_exp"], 1)
                    if C_on and j == 0:
                        wait(act, "x_O", count(1, C, 1, B))
                        wait(act, "x_OT", count(1, C - 1, 1, B))
                        a_.activation(XO, bank[7][:, :], ACT.Copy).then_inc(s["x_Oc"], 1)

            xslots(act, xslot)

            def slot(n, k):
                zu, z_on = part(n, -1, UNITS + 1)
                a, a_on = part(n, 0)
                b, b_on = part(n, 2)
                c, c_on = part(n, 3)
                d, d_on = part(n, 4)
                pb = k % 2

                def square(j):
                    wait(act, "p_qk", count(4, a, j + 1))
                    wait(act, "d_ss", count(1, a - 1, 1))
                    a_.activation(sq[:, 512 * j:512 * j + 512], bank[j % 2][:, :], ACT.Square)\
                        .then_inc(s["a_sq"], 1)

                def copy_T(j):
                    wait(act, "p_tr", count(4, b, j + 1))
                    wait(act, "p_S", count(1, b - 1, 1))
                    a_.activation(qkT[:, 4 * j:4 * j + 4, :], bank[4 + j % 2][:, :].rearrange("p (h q) -> p h q", h=4),
                                  ACT.Copy).then_inc(s["a_tr"], 1)

                def copy_v(e):
                    wait(act, "p_v", count(2, b, e + 1))
                    wait(act, "p_AV", count(2, b - 2, 2))
                    wait(act, f"l_v{pb}", 64 * ((b - 2) // 2) + 64 if isinstance(b, int) else (b >> 1) * 64)
                    a_.activation(vt[:, pb, e, :], bank[e][:, :], ACT.Copy).then_inc(s["a_v"], 1)

                def copy_o(j):
                    wait(act, "p_AV", count(2, c, j + 1))
                    wait(act, "p_y", count(1, c - 1, 1))
                    a_.activation(oT[:, 4 * j:4 * j + 4, :],
                                  bank[4 + j][:, :].rearrange("p (h q) -> p h q", h=4),
                                  ACT.Copy).then_inc(s["a_AV"], 1)

                if a_on:
                    square(0)
                if b_on:
                    copy_T(0)
                    copy_T(1)
                if a_on:
                    square(1)
                if b_on:
                    copy_T(2)
                    copy_T(3)
                if a_on:
                    square(2)
                if z_on:
                    wait(act, "p_zT", count(1, zu, 1, UNITS + 1))
                    wait(act, "p_v", count(2, zu - 4, 2))
                    if isinstance(zu, int) and zu < 4:
                        wait(act, "u_zs", 1)
                    t = zsT[:, (k + 1) % 4, :]
                    a_.activation(t[0:64, :], bank[7][0:64, 0:128], ACT.Copy).then_inc(s["a_zs"], 1)
                    a_.activation(t[64:128, 1:128], bank[7][64:128, 0:127], ACT.Copy).then_inc(s["a_zs"], 1)
                if a_on:
                    square(3)
                if d_on:
                    wait(act, "p_znT", count(1, d, 1))
                    wait(act, "l_gb", 128 * layer_of(d) + 128)
                    wait(act, "p_a", count(1, d - 1, 1))
                    a_.activation(znT[:, :], bank[6][:, 0:128], ACT.Identity, scale=gb[:, 0:1], bias=gb[:, 1:2])\
                        .then_inc(s["a_zn"], 1)
                if c_on:
                    for j in range(2):
                        wait(act, "p_PT", count(2, c, j + 1))
                        wait(act, "p_AV", count(2, c - 1, 2))
                        a_.activation(PT[:, 4 * j:4 * j + 4, :],
                                      bank[4 + j][:, :].rearrange("p (h q) -> p h q", h=4),
                                      ACT.Copy).then_inc(s["a_PT"], 1)
                if b_on:
                    copy_v(0)
                    wait(act, "d_sub", count(1, b, 1))
                    a_.activation(P[:, pb, :], P[:, pb, :], ACT.Exp).then_inc(s["a_exp"], 1)
                if d_on:
                    wait(act, "p_gate", count(1, d, 1))
                    wait(act, "d_h", count(1, d - 1, 1))
                    for j, (_, m) in enumerate(FCH):
                        ins = a_.activation(gl[0:m, j, :], bank[7][0:m, 128 * j:128 * j + 128], ACT.Gelu,
                                            bias=b1c[0:m, 3 + j:4 + j])
                    ins.then_inc(s["a_gelu"], 1)
                if c_on:
                    copy_o(0)
                if b_on:
                    copy_v(1)
                if c_on:
                    copy_o(1)
                act.preload_act_table_set("natural_log_exp_and_others")

            slots(act, slot)

        @block.vector
        def _(dve):
            v_ = nc.vector
            dve.wait_ge(s["l_cst"], 16)
            v_.tensor_copy(identb[:, :], ident).then_inc(s["u_bf"], 1)
            v_.tensor_copy(maskb[:, :], cst[:, C_MASK:C_MASK + 64]).then_inc(s["u_bf"], 1)
            dve.wait_ge(s["l_xw"], 80)
            v_.tensor_copy(xwkr[:, :].rearrange("p (g r d) -> p g r d", g=XG, r=XR),
                           xwk[:, :].rearrange("p (g d) -> p g d", g=XG).unsqueeze(2).to_broadcast([128, XG, XR, XD]))\
                .then_inc(s["u_wkr"], 1)
            dve.wait_ge(s["u_dmc"], 1)
            v_.tensor_scalar(dmT[:, 1, :], dmT[:, 1, :], -1.0, 1e9, ALU.add, ALU.mult).then_inc(s["u_dmc"], 1)
            dve.wait_ge(s["l_x"], 64)
            with dve.Fori(0, B) as b:
                v_.bn_stats(stx[:, bass.ds(b * 6, 6)], z_sb[:, bass.ds(b * E, E)]).then_inc(s["u_st"], 1)
            dve.wait_ge(s["u_st"], B)
            st = stx[:, :].rearrange("p (b c) -> p b c", c=6)
            v_.tensor_tensor(mean0[:, :], st[:, :, 1], st[:, :, 4], ALU.add).then_inc(s["u_ag"], 1)
            v_.tensor_tensor(dif0[:, :], st[:, :, 1], st[:, :, 4], ALU.subtract).then_inc(s["u_ag"], 1)
            v_.tensor_tensor(ve0[:, :], st[:, :, 2], st[:, :, 5], ALU.add).then_inc(s["u_ag"], 1)
            dve.wait_ge(s["u_ag"], 3)
            v_.tensor_scalar(mean0[:, :], mean0[:, :], 0.5, None, ALU.mult).then_inc(s["u_ag"], 1)
            v_.tensor_tensor(dif0[:, :], dif0[:, :], dif0[:, :], ALU.mult).then_inc(s["u_ag"], 1)
            v_.tensor_scalar(ve0[:, :], ve0[:, :], 1.0 / E, LN_EPS, ALU.mult, ALU.add).then_inc(s["u_ag"], 1)
            dve.wait_ge(s["u_ag"], 6)
            v_.scalar_tensor_tensor(ve0[:, :], dif0[:, :], 0.25, ve0[:, :], ALU.mult, ALU.add).then_inc(s["u_ve"], 1)
            dve.wait_ge(s["u_dmc"], 2)
            dve.wait_ge(s["u_rstd"], 1)
            dve.wait_ge(s["u_ctc"], 1)
            dmf = dmT[:, :, :].rearrange("p c b -> p (c b)")

            def rows(A, pA):
                wait(dve, "x_A1", count(1, A - 2, 1, B))
                v_.tensor_scalar(xn[:, pA, :], z_sb[:, bass.ds(A * E, E)], mean0[:, bass.ds(A, 1)],
                                 rstd0[:, bass.ds(A, 1)], ALU.subtract, ALU.mult).then_inc(s["x_xn"], 1)
                v_.tensor_scalar(td[:, pA, 0:S], tri, dmf[:, bass.ds(A, 1)], None, ALU.mult)\
                    .then_inc(s["x_td"], 1)
                v_.tensor_scalar(td[:, pA, S:2 * S], ident, dmf[:, bass.ds(A + B, 1)], None, ALU.mult)\
                    .then_inc(s["x_td"], 1)

            rows(0, 0)

            def xslot(n, k):
                A1, A1_on = part(n, -1, B)
                A, A_on = part(n, 0, B)
                Bt, B_on = part(n, 1, B)
                D, D_on = part(n, 3, B)
                pA, pB = k % 2, (k - 1) % 2
                xc = bass.ds(D * E, E)
                if D_on:
                    wait(dve, "x_OT", count(1, D, 1, B))
                    o4 = bank[7][:, :].rearrange("p (r g d) -> p r g d", r=XR, g=XG)
                    v_.reciprocal(xrs[:, :].rearrange("p (g r) -> p r g", g=XG), o4[:, :, :, XD]).then_inc(s["x_rs"], 1)
                    wait(dve, "x_rs", count(1, D, 1, B))
                    wait(dve, "x_aT", count(1, D - 1, 1, B))
                    at = attn[:, :, :].rearrange("p (g r) d -> p r g d", g=XG)
                    rs = xrs[:, :].rearrange("p (g r) -> p r g", g=XG)
                    for r in range(XR):
                        ins = v_.tensor_tensor(at[:, r, :, :], o4[:, r, :, 0:XD],
                                               rs[:, r, :].unsqueeze(2).to_broadcast([128, XG, XD]), ALU.mult)
                    ins.then_inc(s["x_attn"], 1)
                if A_on:
                    wait(dve, "x_A1", count(1, A, 1, B))
                    wait(dve, "x_ln", count(1, A - 1, 1, B))
                    wait(dve, "x_cxT", count(1, A, 1, B))
                    wait(dve, "x_bias", count(1, A - 1, 1, B))
                    v_.tensor_copy(mbr[:, :], bank[6][:, 384:512]).then_inc(s["x_dabs"], 1)
                    v_.tensor_scalar(dif[:, :], bank[6][:, 256:384], ctT[:, bass.ds(A, 1)], None,
                                     ALU.subtract).then_inc(s["x_dabs"], 1)
                    wait(dve, "x_dabs", count(3, A, 2, B))
                    v_.scalar_tensor_tensor(dabs[:, :], dif[:, :], -1.0, dif[:, :], ALU.mult, ALU.max)\
                        .then_inc(s["x_dabs"], 1)
                if B_on:
                    for j in range(2):
                        wait(dve, "x_S", count(4, Bt, 2 * j + 2, B))
                        wait(dve, "x_PT", count(4, Bt - 2, 4, B))
                        wait(dve, "x_bias", count(1, Bt, 1, B))
                        for i in range(2):
                            v_.tensor_tensor(
                                XP[:, pB, 1024 * j + 512 * i:1024 * j + 512 * i + 512]
                                .rearrange("p (h q) -> p h q", q=S),
                                bank[2 * j + i][:, :].rearrange("p (h q) -> p h q", q=S),
                                bias[:, pB, :].unsqueeze(1).to_broadcast([128, 4, S]), ALU.add)\
                                .then_inc(s["x_add"], 1)
                        pr = XP[:, pB, 1024 * j:1024 * j + 1024].rearrange("p (h q) -> p h q", q=S)
                        wait(dve, "x_add", count(4, Bt, 2 * j + 2, B))
                        wait(dve, "x_sub", count(4, Bt - 1, 2 * j + 2, B))
                        v_.tensor_reduce(xmax[:, 8 * j:8 * j + 8], pr, AX.X, ALU.max).then_inc(s["x_max"], 1)
                if D_on:
                    wait(dve, "x_y", count(1, D, 1, B))
                    v_.tensor_tensor(x1cur[:, :], bank[4][:, 0:128], z_sb[:, xc], ALU.add).then_inc(s["x_x1"], 1)
                    wait(dve, "x_x1", count(1, D, 1, B))
                    v_.bn_stats(stats[:, 0:6], x1cur[:, :]).then_inc(s["x_bn"], 1)
                    wait(dve, "x_bn", count(1, D, 1, B))
                    v_.tensor_copy(x1_sb[:, xc], x1cur[:, :]).then_inc(s["x_store"], 1)
                    v_.bn_aggr(mv[:, :], stats[:, 0:6]).then_inc(s["x_agg"], 1)
                    wait(dve, "x_agg", count(1, D, 1, B))
                    v_.tensor_scalar(ve[:, 0:1], mv[:, 1:2], LN_EPS, None, ALU.add).then_inc(s["x_ve"], 1)
                if A_on:
                    wait(dve, "x_ln", count(1, A, 1, B))
                    wait(dve, "x_dabs", count(3, A, 3, B))
                    v_.scalar_tensor_tensor(bias[:, pA, :], lnt[:, :], xtwc[:, 0:1], mbr[:, :], ALU.mult, ALU.add)\
                        .then_inc(s["x_bias"], 1)
                    wait(dve, "x_A2", count(1, A, 1, B))
                    wait(dve, "x_vaug", count(1, A, 1, B))
                    wait(dve, "x_S", count(4, A - 2, 4, B))
                    v_.tensor_tensor(kblk[:, pA, :].rearrange("p (r t) -> p r t", r=XR),
                                     bank[6][:, 128:256].unsqueeze(1).to_broadcast([128, XR, S]),
                                     blk.unsqueeze(2).to_broadcast([128, XR, S]), ALU.mult).then_inc(s["x_kblk"], 1)
                if A1_on:
                    rows(A1, (k + 1) % 2)
                if D_on:
                    wait(dve, "x_rstd", count(1, D, 1, B))
                    v_.tensor_scalar(z_sb[:, xc], x1cur[:, :], mv[:, 0:1], rstd[:, 0:1], ALU.subtract, ALU.mult)\
                        .then_inc(s["z_ready"], 1)

            xslots(dve, xslot)

            def slot(n, k):
                a, a_on = part(n, 0)
                b, b_on = part(n, 2)
                c, c_on = part(n, 3)
                d, d_on = part(n, 4)
                pa, pb, pd = k % 2, k % 2, k % 2

                def rotary(j):
                    wait(dve, "a_sq", count(4, a, j + 1))
                    wait(dve, "g_add", count(4, a - 1, j + 1))
                    if j == 0:
                        wait(dve, "l_rot", 16 * layer_of(a) + 16)
                    o = 128 * (j // 2)
                    src = bank[j % 2][:, :].rearrange("p (h d) -> p h d", d=DH)
                    for t, r in ((ta, rot[:, o:o + 64]), (tb, rot[:, o + 64:o + 128])):
                        ins = v_.tensor_tensor(t[:, 512 * j:512 * j + 512].rearrange("p (h d) -> p h d", d=DH), src,
                                               r.unsqueeze(1).to_broadcast([128, 8, DH]), ALU.mult)
                    ins.then_inc(s["d_rot"], 1)

                if d_on:
                    wait(dve, "p_y", count(1, d, 1))
                    wait(dve, "p_zsh", count(1, d - 2, 1))
                    wait(dve, "g_zmb", count(1, d - 2, 1))
                    v_.tensor_tensor(zm[:, pd, :], bank[7][:, 384:512], z_sb[:, cols(d)], ALU.add)\
                        .then_inc(s["d_zm"], 1)
                if a_on:
                    rotary(0)
                if d_on:
                    wait(dve, "p_zsh", count(1, d, 1))
                    v_.bn_stats(stats[:, 0:6], bank[6][:, 0:128]).then_inc(s["d_bn"], 1)
                    wait(dve, "d_bn", count(1, d, 1))
                    dve.nop(nofuse=True)
                    v_.bn_aggr(mv[:, :], stats[:, 0:6]).then_inc(s["d_agg"], 1)
                    wait(dve, "d_agg", count(1, d, 1))
                    v_.tensor_scalar(ve[:, pd:pd + 1], mv[:, 1:2], LN_EPS, None, ALU.add).then_inc(s["d_ve"], 1)
                if a_on:
                    rotary(1)
                if d_on:
                    wait(dve, "g_rstd", count(1, d, 1))
                    wait(dve, "p_znT", count(1, d - 1, 1))
                    v_.tensor_scalar(zn[:, :], bank[6][:, 0:128], mv[:, 0:1], rstd[:, pd:pd + 1],
                                     ALU.subtract, ALU.mult).then_inc(s["d_zn"], 1)
                if a_on:
                    rotary(2)
                if b_on:
                    wait(dve, "p_S", count(1, b, 1))
                    wait(dve, "p_PT", count(2, b - 2, 2))
                    for e in range(2):
                        mx = rowmax[:, 8 * e:8 * e + 8]
                        v_.tensor_reduce(mx, SC[e][:, :].rearrange("p (h t) -> p h t", t=DH), AX.X, ALU.max)\
                            .then_inc(s["d_max"], 1)
                    for e in range(2):
                        mx = rowmax[:, 8 * e:8 * e + 8]
                        wait(dve, "d_max", count(2, b, e + 1))
                        ins = v_.tensor_tensor(P[:, pb, :].rearrange("p (h e t) -> p h e t", e=2, t=DH)[:, :, e, :],
                                               SC[e][:, :].rearrange("p (h t) -> p h t", t=DH),
                                               mx.unsqueeze(2).to_broadcast([128, PAIRS, DH]), ALU.subtract)
                    ins.then_inc(s["d_sub"], 1)
                if a_on:
                    rotary(3)
                    wait(dve, "g_pow", count(1, a - 2, 1))
                    v_.tensor_reduce(ss[:, pa, :], sq[:, :].rearrange("p (h d) -> p h d", d=DH), AX.X, ALU.add)\
                        .then_inc(s["d_sumsq"], 1)
                    wait(dve, "d_sumsq", count(1, a, 1))
                    v_.tensor_scalar(ss[:, pa, :], ss[:, pa, :], NORM_MIN2, None, ALU.max).then_inc(s["d_ss"], 1)
                if d_on:
                    wait(dve, "p_a", count(1, d, 1))
                    wait(dve, "a_gelu", count(1, d, 1))
                    wait(dve, "p_y2", count(1, d - 1, 1))
                    for j, (_, m) in enumerate(FCH):
                        ins = v_.scalar_tensor_tensor(hT[0:m, j, :], bank[6][0:m, 128 * j:128 * j + 128],
                                                      b1c[0:m, j:j + 1], gl[0:m, j, :], ALU.add, ALU.mult)
                    ins.then_inc(s["d_h"], 1)
                if b_on:
                    wait(dve, "a_exp", count(1, b, 1))
                    pr = P[:, pb, :].rearrange("p (h t) -> p h t", t=DH)
                    v_.tensor_reduce(rowsum[:, 0, :], pr, AX.X, ALU.add).then_inc(s["d_sum"], 1)
                    wait(dve, "d_sum", count(1, b, 1))
                    v_.reciprocal(rowsum[:, 1, :], rowsum[:, 0, :]).then_inc(s["d_rec"], 1)
                    wait(dve, "d_rec", count(1, b, 1))
                    v_.tensor_tensor(pr, pr, rowsum[:, 1, :].unsqueeze(2).to_broadcast([128, HEADS, DH]),
                                     ALU.mult).then_inc(s["d_P"], 1)
                if d_on:
                    wait(dve, "p_y2", count(1, d, 1))
                    wait(dve, "g_zmb", count(1, d, 1))
                    v_.tensor_tensor(z_sb[:, cols(d)], bank[6][:, 384:512], zmb[:, pd, :], ALU.add)\
                        .then_inc(s["z_ready"], 1)

            slots(dve, slot)
            dve.wait_ge(s["z_ready"], B + UNITS)
            dve.wait_ge(s["x_store"], B)
            for c in range(8):
                cc = slice(512 * c, 512 * c + 512)
                v_.tensor_tensor(x1_sb[:, cc], x1_sb[:, cc], z_sb[:, cc], ALU.add).then_inc(s["d_out"], 1)

        @block.tensor
        def _(pe):
            t_ = nc.tensor
            pe.wait_ge(s["l_cst"], 16)
            pe.wait_ge(s["l_dm"], 32)
            t_.transpose(bank[6][:, 0:32], dm[:, 0, :], ident[0:32, 0:32])
            t_.transpose(bank[6][:, 32:64], dm[:, 1, :], ident[0:32, 0:32]).then_inc(s["u_dmT"], 1)
            pe.wait_ge(s["u_dmc"], 1)
            t_.matmul(bank[6][:, 64:96], tri, dmT[:, 0, :], start=True, stop=True).then_inc(s["u_ct"], 1)
            pe.wait_ge(s["u_ctc"], 1)
            pe.wait_ge(s["u_ones"], 1)
            pe.wait_ge(s["l_xw"], 80)
            pe.wait_ge(s["u_wkr"], 1)

            def xslot(n, k):
                A, A_on = part(n, 0, B)
                Bt, B_on = part(n, 1, B)
                C, C_on = part(n, 2, B)
                D, D_on = part(n, 3, B)
                pA, pB, pC = k % 2, (k - 1) % 2, k % 2
                if D_on:
                    wait(pe, "x_Oc", count(1, D, 1, B))
                    for r in range(XR):
                        ins = t_.transpose(bank[7][:, 128 * r:128 * r + 128], XO[:, 128 * r:128 * r + 128], ident)
                    ins.then_inc(s["x_OT"], 1)
                if A_on:
                    wait(pe, f"l_ctx{pA}", 16 * (A // 2) + 16 if isinstance(A, int) else (A >> 1) * 16 + 16)
                    wait(pe, "x_xn", count(1, A, 1, B))
                    wait(pe, "x_td", count(2, A, 2, B))
                    wait(pe, "x_kblk", count(1, A - 1, 1, B))
                    wait(pe, "x_vaug", count(1, A - 1, 1, B))
                    t_.transpose(bank[6][:, 0:128], ctxb[:, pA, :], ident)
                    t_.transpose(bank[6][:, 128:256], xn[:, pA, :], ident)
                    t_.matmul(bank[6][:, 256:512], ones[:, :], td[:, pA, :], start=True, stop=True)\
                        .then_inc(s["x_A1"], 1)
                if B_on:
                    wait(pe, "x_q", count(1, Bt, 1, B))
                    wait(pe, "x_kblk", count(1, Bt, 1, B))
                    for gr in range(XG):
                        wait(pe, "x_add", count(4, Bt - 1, gr + 1, B))
                        r = slice(32 * gr, 32 * gr + 32)
                        t_.matmul(bank[gr][:, :], qT[r, pB, :], kblk[r, pB, :], start=True, stop=True)\
                            .then_inc(s["x_S"], 1)
                if D_on:
                    wait(pe, "x_attn", count(1, D, 1, B))
                    t_.transpose(bank[7][:, 0:128], attn[:, :, :].rearrange("p h d -> p (h d)"), ident)\
                        .then_inc(s["x_aT"], 1)
                if C_on:
                    wait(pe, "x_x1", count(1, D - 1, 1, B))
                    for j in range(4):
                        wait(pe, "x_exp", count(2, C, j // 2 + 1, B))
                        wait(pe, "x_PTc", count(4, C, j - 1, B) if j >= 2 else count(4, C - 1, j + 3, B))
                        for h in range(4):
                            hh = 4 * j + h
                            ins = t_.transpose(bank[4 + j % 2][:, 128 * h:128 * h + 128],
                                               XP[:, pC, 128 * hh:128 * hh + 128], ident)
                        ins.then_inc(s["x_PT"], 1)
                if A_on:
                    wait(pe, "x_cxT", count(1, A, 1, B))
                    wait(pe, "x_dabs", count(3, A, 2, B))
                    t_.matmul(bank[6][:, 0:128], xwq[:, :], cxT[:, pA, S:2 * S], start=True, stop=True)
                    t_.matmul(bank[6][:, 128:256], xwkr[:, :], cxT[:, pA, 0:S], start=True, stop=True)
                    t_.matmul(bank[6][:, 256:288], cxT[:, pA, 0:S], xwv[:, :], start=True, stop=True)\
                        .then_inc(s["x_A2"], 1)
                if D_on:
                    wait(pe, "x_aTc", count(1, D, 1, B))
                    wait(pe, "x_PTc", count(4, C, 3, B))
                    t_.matmul(bank[4][:, 0:128], attnT[:, :], xwo[:, :], start=True, stop=True)\
                        .then_inc(s["x_y"], 1)
                if C_on:
                    wait(pe, "x_PTc", count(4, C, 4, B))
                    wait(pe, "x_vaug", count(1, C, 1, B))
                    wait(pe, "x_aTc", count(1, D, 1, B))
                    for gr in range(XG):
                        ins = t_.matmul(bank[7][32 * gr:32 * gr + 32, :], vaug[:, pC, gr, :],
                                        XPT[:, 4 * gr:4 * gr + 4, :], start=True, stop=True)
                    ins.then_inc(s["x_O"], 1)

            xslots(pe, xslot)
            pe.wait_ge(s["u_bf"], 2)
            pe.wait_ge(s["x_x1"], B)

            def slot(n, k):
                zu, z_on = part(n, -1, UNITS + 1)
                a, a_on = part(n, 0)
                b, b_on = part(n, 2)
                c, c_on = part(n, 3)
                d, d_on = part(n, 4)
                pb, pc, pd = k % 2, (k - 3) % 2, k % 2

                def proj_qk(j):
                    if j == 0:
                        wait(pe, "a_zs", count(2, a, 2, UNITS + 1))
                        wait(pe, "l_wqk", 16 * layer_of(a) + 16)
                    if j < 2:
                        wait(pe, "d_rot", count(4, a - 1, j + 3))
                        wait(pe, "a_v", count(2, b - 1, j + 1))
                    else:
                        wait(pe, "d_rot", count(4, a, j - 1))
                    t_.matmul(bank[j % 2][:, :], zsT[:, k % 4, :], wqkv[:, 512 * j:512 * j + 512],
                              start=True, stop=True).then_inc(s["p_qk"], 1)

                def proj_v(e):
                    if e == 0:
                        wait(pe, "l_wv", 16 * layer_of(b) + 16)
                    wait(pe, "d_rot", count(4, a, e + 3))
                    wait(pe, "a_v", count(2, b - 1, e + 1))
                    wv = wqkv[:, 2 * INNER:].rearrange("i (p e d) -> i p e d", e=2, d=DH)
                    t_.matmul(bank[e][:, :], zsT[:, (k + 2) % 4, :], wv[:, :, e, :], start=True, stop=True)\
                        .then_inc(s["p_v"], 1)

                def transpose_qk(j):
                    wait(pe, "g_qk", count(4, b, j + 1))
                    if j < 2:
                        wait(pe, "a_tr", count(4, b - 1, j + 3))
                        wait(pe, "a_AV", count(2, c - 1, j + 1))
                    else:
                        wait(pe, "a_tr", count(4, b, j - 1))
                    for p in range(4):
                        ins = t_.transpose(bank[4 + j % 2][:, 128 * p:128 * p + 128],
                                           qk[:, pb, 512 * j + 128 * p:512 * j + 128 * p + 128], ident)
                    ins.then_inc(s["p_tr"], 1)

                def attend(j):
                    wait(pe, "a_PT", count(2, c, j + 1))
                    if j == 0:
                        wait(pe, f"l_v{pc}", 64 * (c // 2) + 64 if isinstance(c, int) else (c >> 1) * 64 + 64)
                        wait(pe, "a_v", count(2, c, 2))
                    pe.nop(nofuse=True)
                    for p in range(4):
                        hp = 4 * j + p
                        hc = slice(64 * hp, 64 * hp + 64)
                        for q0, nq, even, odd in ((0, 64, vt[0:64, pc, 0, hc], vs[64:128, pc, 1, hc]),
                                                  (64, 32, vs[0:64, pc, 0, hc], vs[64:128, pc, 0, hc]),
                                                  (96, 32, vs[0:64, pc, 1, hc], vt[64:128, pc, 1, hc])):
                            for e, ve_ in enumerate((even, odd)):
                                r = slice(64 * e, 64 * e + 64)
                                ins = t_.matmul(bank[4 + j][r, 128 * p + q0:128 * p + q0 + nq], ve_,
                                                PT[r, hp, q0:q0 + nq], start=True, stop=True)
                    ins.then_inc(s["p_AV"], 1)

                if a_on:
                    proj_qk(0)
                if b_on:
                    transpose_qk(0)
                    transpose_qk(1)
                if d_on:
                    wait(pe, "d_zm", count(1, d, 1))
                    wait(pe, "z_ready", (count(1, d - 1, 1) if isinstance(d, int) else d) + B)
                    t_.matmul(bank[6][:, 0:64], ident, zm[:, pd, 0:64], start=True, stop=True)
                    t_.matmul(bank[6][:, 64:128], shift, zm[:, pd, 64:128], start=True, stop=True)\
                        .then_inc(s["p_zsh"], 1)
                if a_on:
                    proj_qk(1)
                if b_on:
                    transpose_qk(2)
                    transpose_qk(3)
                if a_on:
                    proj_qk(2)
                if z_on:
                    wait(pe, "g_z", count(1, zu, 1, UNITS + 1))
                    wait(pe, "d_zm", count(1, d, 1))
                    wait(pe, "a_zs", count(2, zu - 1, 2, UNITS + 1))
                    t_.transpose(bank[7][:, 0:128], zcur[:, (k + 1) % 2, :], ident).then_inc(s["p_zT"], 1)
                if b_on:
                    wait(pe, "a_tr", count(4, b, 4))
                    wait(pe, "d_sub", count(1, b - 1, 1))
                    for e in range(2):
                        t_.matmul(SC[e][:, :], identb[:, :], maskb[:, :].unsqueeze(1).to_broadcast([128, PAIRS, DH]),
                                  start=True, stop=False, skip_group_check=True)
                    for p in range(PAIRS):
                        for w in range(NW):
                            k0 = WIN * max(0, w - 1)
                            for e in range(2):
                                r = slice(64 * e, 64 * e + 64)
                                ins = t_.matmul(SC[e][WIN * w:WIN * w + WIN, 64 * p:64 * p + 64],
                                                qkT[r, p, WIN * w:WIN * w + WIN], qkT[r, PAIRS + p, k0:k0 + 64],
                                                start=False, stop=p == PAIRS - 1, skip_group_check=True)
                    ins.then_inc(s["p_S"], 1)
                if a_on:
                    proj_qk(3)
                if d_on:
                    wait(pe, "d_zn", count(1, d, 1))
                    t_.transpose(bank[6][:, 0:128], zn[:, :], ident).then_inc(s["p_znT"], 1)
                if c_on:
                    for j in range(2):
                        wait(pe, "d_P", count(1, c, 1))
                        wait(pe, "a_tr", count(4, b, 3 + j))
                        wait(pe, "a_AV", count(2, c - 1, 2))
                        for p in range(4):
                            hp = 4 * j + p
                            ins = t_.transpose(bank[4 + j][:, 128 * p:128 * p + 128],
                                               P[:, pc, 128 * hp:128 * hp + 128], ident)
                        ins.then_inc(s["p_PT"], 1)
                if b_on:
                    proj_v(0)
                if d_on:
                    wait(pe, "a_zn", count(1, d, 1))
                    wait(pe, "l_w1", 16 * layer_of(d) + 16)
                    wait(pe, "a_zs", count(2, zu, 2, UNITS + 1))
                    for j, (o, m) in enumerate(FCH):
                        ins = t_.matmul(bank[7][0:m, 128 * j:128 * j + 128], w1[:, FF + o:FF + o + m], znT[:, :],
                                        start=True, stop=True)
                    ins.then_inc(s["p_gate"], 1)
                    for j, (o, m) in enumerate(FCH):
                        ins = t_.matmul(bank[6][0:m, 128 * j:128 * j + 128], w1[:, o:o + m], znT[:, :],
                                        start=True, stop=True)
                    ins.then_inc(s["p_a"], 1)
                if c_on:
                    attend(0)
                if b_on:
                    proj_v(1)
                if c_on:
                    attend(1)
                if d_on:
                    wait(pe, "d_h", count(1, d, 1))
                    wait(pe, "l_w2", 48 * layer_of(d) + 48)
                    for j, (_, m) in enumerate(FCH):
                        ins = t_.matmul(bank[6][:, 384:512], hT[0:m, j, :], w2[0:m, j, :], start=j == 0, stop=j == 2)
                    ins.then_inc(s["p_y2"], 1)
                if c_on:
                    wait(pe, "a_AV", count(2, c, 2))
                    wait(pe, "l_wo", 16 * layer_of(c) + 16)
                    wait(pe, "a_gelu", count(1, d, 1))
                    wait(pe, "a_zs", count(2, zu, 2, UNITS + 1))
                    for p in range(PAIRS):
                        ins = t_.matmul(bank[7][:, 384:512], oT[:, p, :], wo[:, p, :], start=p == 0,
                                        stop=p == PAIRS - 1)
                    ins.then_inc(s["p_y"], 1)

            slots(pe, slot)


_INS = ['x', 'ctx_1024', 'fside_BxS2_0', 'mask_BxS2_ff1', 'L0_xattn_Wq', 'L0_xattn_Wk', 'L0_xattn_Wv', 'L0_xattn_Wo',
        'L0_xattn_time_bias_weight', 'L0_ffn_Wqkv', 'L0_ffn_q_scale', 'L0_ffn_k_scale', 'L0_ffn_Wo', 'L0_ffn_ln_g',
        'L0_ffn_ln_b', 'L0_ffn_W1', 'L0_ffn_b1', 'L0_ffn_W2', 'L0_ffn_b2']


def kernel(**inputs):
    import concourse.bacc as bacc
    from concourse.bass_utils import run_bass_kernel_spmd

    nc = bacc.Bacc("TRN2", target_bir_lowering=False, num_devices=1)
    arrays, args = {}, []
    for name in _INS:
        a = np.ascontiguousarray(inputs[name])
        if a.ndim == 0 or name == 'L0_xattn_time_bias_weight':
            a = a.reshape(1)
        arrays[name] = a
    arrays["consts"] = constants()
    for name, a in arrays.items():
        args.append(nc.dram_tensor(name, a.shape, mybir.dt.from_np(a.dtype), kind="ExternalInput").ap())
    args.append(nc.dram_tensor("out", (B, S, E), F32, kind="ExternalOutput").ap())
    build(nc, *args)
    r = run_bass_kernel_spmd(nc, [arrays], core_ids=[0])
    return r.results[0]["out"]
```

```python
from contextlib import ExitStack

import numpy as np

import concourse.bass as bass
from concourse import mybir

F32 = mybir.dt.float32
BF16 = mybir.dt.bfloat16
ALU = mybir.AluOpType
ACT = mybir.ActivationFunctionType
AX = mybir.AxisListType

B, S, E = 32, 128, 128
XH, XG, XD = 16, 4, 8
XR = XH // XG
XSCALE = 1.0 / float(XD) ** 0.5
DEPTH, HEADS, DH, WIN = 6, 16, 64, 32
INNER = HEADS * DH
PAIRS = HEADS // 2
NW = S // WIN
FF = int(E * 4 * 2 / 3)
FCH = [(0, 128), (128, 128), (256, FF - 256)]
QK_SCALE = 8.0
UNITS = DEPTH * B
LN_EPS = 1e-5
NORM_MIN2 = 1e-24
MASKED = -(2.0 ** 120)

C_ID, C_SH, C_TRI, C_ROT, C_MASK, C_BLK, C_END = 0, 128, 256, 384, 640, 704, 708


def constants():
    c = np.zeros((128, C_END), np.float32)
    r = np.arange(128)
    c[:, C_ID:C_ID + 128] = np.eye(128)
    c[r[:-1], C_SH + 1 + r[:-1]] = 1.0
    c[:, C_TRI:C_TRI + 128] = r[:, None] <= r[None, :]
    half = np.arange(0, DH, 2, dtype=np.float32)
    inv = (1.0 / np.float32(10000.0) ** (half / np.float32(DH))).astype(np.float32)
    t = np.arange(S, dtype=np.float32)
    f = (t[:, None] * inv[None, :]).astype(np.float32)
    base = (half + np.float32(0.4 * DH)) / np.float32(1.4 * DH)
    scale = (base[None, :] ** ((t - S // 2) / (WIN // 2))[:, None]).astype(np.float32)
    cos, sin = np.cos(f).astype(np.float32), np.sin(f).astype(np.float32)
    for k, s in enumerate((scale * np.float32(QK_SCALE), np.float32(1.0) / scale)):
        o = C_ROT + 128 * k
        c[:, o:o + 64] = np.concatenate([cos * s, cos * s], 1)
        c[:, o + 64:o + 128] = np.concatenate([sin * s, -(sin * s)], 1)
    w = r // WIN
    key = np.where(w == 0, 0, (w - 1) * WIN)[:, None] + np.arange(64)[None, :]
    ok = (key <= r[:, None]) & (key + WIN >= r[:, None])
    c[:, C_MASK:C_MASK + 64] = np.where(ok, 0.0, MASKED)
    c[:, C_BLK:C_BLK + XR] = (r[:, None] // XD) % XR == np.arange(XR)[None, :]
    return c


def build(nc, x, ctx, deltas, mask, xWq, xWk, xWv, xWo, xtw, Wqkv, qs, ks, Wo, lng, lnb, W1, b1, W2, b2, consts, out):
    es = ExitStack()
    with es:
        def sb(name, shape, dt=F32):
            return es.enter_context(nc.sbuf_tensor(name, shape, dt))

        def ps(name):
            return es.enter_context(nc.psum_tensor(name, [128, 512], F32))

        def sem(name):
            return es.enter_context(nc.semaphore(name))

        cst = sb("cst", [128, C_END])
        ident = cst[:, C_ID:C_ID + 128]
        shift = cst[:, C_SH:C_SH + 128]
        tri = cst[:, C_TRI:C_TRI + 128]
        rotc = cst[:, C_ROT:C_ROT + 256]
        blk = cst[:, C_BLK:C_BLK + XR]
        identb = sb("identb", [128, 128], BF16)
        maskb = sb("maskb", [128, 64], BF16)
        z_sb = sb("z_sb", [128, B * E])
        x1_sb = sb("x1_sb", [128, B * E])
        zv = z_sb[:, :].rearrange("p (b e) -> p b e", b=B)
        x1v = x1_sb[:, :].rearrange("p (b e) -> p b e", b=B)
        wqkv = sb("wqkv", [128, 3 * INNER])
        wo = sb("wo", [128, PAIRS, E])
        w1 = sb("w1", [128, 2 * FF])
        w2 = sb("w2", [128, 3, E])
        gb = sb("gb", [128, 2])
        b1c = sb("b1c", [128, 6])
        b2r = sb("b2r", [128, E])
        rot = sb("rot", [128, 4 * DH])
        rot_all = sb("rot_all", [128, DEPTH, 4 * DH])
        qks = sb("qks", [128, 2, DEPTH * DH])
        zcur = sb("zcur", [128, 2, E])
        zsT = sb("zsT", [128, 4, S])
        sq = sb("sq", [128, 2 * INNER])
        ta = sb("ta", [128, 2 * INNER])
        tb = sb("tb", [128, 2 * INNER])
        qk = sb("qk", [128, 2, 2 * INNER])
        ss = sb("ss", [128, 2, 2 * HEADS])
        rn = sb("rn", [128, 2, 2 * HEADS])
        half_neg = sb("half_neg", [128, 2 * HEADS])
        qT2 = sb("qT2", [128, PAIRS, S])
        kz = sb("kz", [128, PAIRS, 2, S])
        P = sb("P", [128, 2, HEADS * DH])
        rowmax = sb("rowmax", [128, HEADS])
        rowsum = sb("rowsum", [128, 2, HEADS])
        pz = sb("pz", [128, PAIRS, 2, S])
        vt = sb("vt", [128, 2, 2, INNER // 2])
        vs = sb("vs", [128, 2, 3, INNER // 2])
        oT = sb("oT", [128, PAIRS, S])
        zm = sb("zm", [128, 2, E])
        zmb = sb("zmb", [128, 2, E])
        stats = sb("stats", [128, 8])
        mv = sb("mv", [128, 2])
        ve = sb("ve", [128, 2])
        rstd = sb("rstd", [128, 2])
        zn = sb("zn", [128, E])
        znT = sb("znT", [128, S])
        gl = sb("gl", [128, 3, S])
        hT = sb("hT", [128, 3, S])
        xwq = sb("xwq", [128, E])
        xwk = sb("xwk", [128, XG * XD])
        xwkr = sb("xwkr", [128, E])
        xwv = sb("xwv", [128, XG * XD])
        xwo = sb("xwo", [128, E])
        xtwc = sb("xtwc", [128, 1])
        dm = sb("dm", [32, 2, S])
        dmT = sb("dmT", [128, 2, B])
        ctT = sb("ctT", [128, B])
        ones = sb("ones", [128, 128])
        stx = sb("stx", [128, B * 6])
        mean0 = sb("mean0", [128, B])
        dif0 = sb("dif0", [128, B])
        ve0 = sb("ve0", [128, B])
        rstd0 = sb("rstd0", [128, B])
        ctxb = sb("ctxb", [128, 2, E])
        xn = sb("xn", [128, 2, E])
        td = sb("td", [128, 2, 2 * S])
        cxT = sb("cxT", [128, 2, 2 * S])
        qT = sb("qT", [128, 2, S])
        kblk = sb("kblk", [128, 2, XR * S])
        vaug = sb("vaug", [128, 2, XG, 32])
        dif = sb("dif", [128, S])
        x1cur = sb("x1cur", [128, E])
        dabs = sb("dabs", [128, S])
        mbr = sb("mbr", [128, S])
        lnt = sb("lnt", [128, S])
        bias = sb("bias", [128, 2, S])
        xmax = sb("xmax", [128, XH])
        xrs = sb("xrs", [128, XH])
        attn = sb("attn", [128, XH, XD])
        attnT = sb("attnT", [128, S])
        XP = qk
        XPT = ta[:, :].rearrange("p (h q) -> p h q", q=S)
        XO = sq[:, 0:512]

        bank = [ps(f"bank{i}") for i in range(8)]
        SC = bank[2:4]

        names = [
            "l_cst", "l_x", "l_xw", "l_dm", "l_ctx0", "l_ctx1", "l_qks", "l_wqk", "l_wv", "l_wo", "l_w1", "l_w2",
            "l_gb", "l_b2", "l_rot", "l_v0", "l_v1",
            "u_bf", "u_ones", "u_wkr", "u_rotq", "u_dmT", "u_dmc", "u_ct", "u_ctc", "u_st", "u_ag", "u_ve", "u_rstd",
            "u_negh", "u_kz", "u_vz", "u_v1", "u_zs",
            "x_xn", "x_td", "x_A1", "x_cxT", "x_dabs", "x_ln", "x_bias", "x_A2", "x_q", "x_kblk", "x_vaug", "x_S",
            "x_add", "x_max", "x_sub", "x_exp", "x_PT", "x_PTc", "x_O", "x_Oc", "x_OT", "x_rs", "x_attn", "x_aT",
            "x_aTc", "x_y", "x_x1", "x_store", "x_bn", "x_agg", "x_ve", "x_rstd", "z_ready",
            "p_zT", "p_qk", "p_v", "p_tr", "p_S", "p_PT", "p_AV", "p_y", "p_zsh", "p_znT", "p_gate", "p_a", "p_y2",
            "a_zs", "a_sq", "a_tr", "a_exp", "a_PT", "a_AV", "a_v", "a_zn", "a_gelu",
            "d_rot", "d_sumsq", "d_ss", "d_max", "d_sub", "d_sum", "d_rec", "d_P", "d_zm", "d_bn", "d_agg", "d_ve", "d_zn",
            "d_h", "d_out",
            "g_z", "g_add", "g_pow", "g_qk", "g_rstd", "g_zmb",
            "out_done",
        ]
        s = {n: sem(n) for n in names}

        def count(per_unit, unit, j, total=UNITS):
            if isinstance(unit, int):
                if unit < 0:
                    return 0
                if unit >= total:
                    return per_unit * total
            return unit * per_unit + j

        def wait(eng, name, value):
            if not (isinstance(value, int) and value <= 0):
                eng.wait_ge(s[name], value)

        def edge(eng, unit, name, value):
            if isinstance(unit, int):
                wait(eng, name, value)

        def layer_of(unit):
            return unit // B if isinstance(unit, int) else unit >> 5

        def cols(unit):
            return bass.ds((unit & (B - 1)) * E, E)

        LOOP0, UNROLL = 8, 4
        LOOP1 = UNITS - 4

        def slots(eng, body):
            for n in range(-2, LOOP0):
                body(n, n)
            with eng.Fori(0, (LOOP1 - LOOP0) // UNROLL) as i:
                for k in range(UNROLL):
                    body(i * UNROLL + (LOOP0 + k), LOOP0 + k)
            for n in range(LOOP1, UNITS + 4):
                body(n, n)

        def part(n, lag, total=UNITS):
            u = n - lag
            return u, (not isinstance(u, int)) or 0 <= u < total

        def xslots(eng, body):
            for n in range(0, 4):
                body(n, n)
            with eng.Fori(0, (B - 6) // 2) as i:
                for k in range(2):
                    body(i * 2 + (4 + k), 4 + k)
            for n in range(B - 2, B + 3):
                body(n, n)

        block = es.enter_context(nc.Block())

        @block.sync
        def _(sp):
            sp.dma_start(cst[:, :], consts).then_inc(s["l_cst"], 16)
            sp.dma_start(dm[:, 0, :], deltas).then_inc(s["l_dm"], 16)
            sp.dma_start(dm[:, 1, :], mask).then_inc(s["l_dm"], 16)
            xr = x.rearrange("b s e -> s b e")
            for c in range(4):
                sp.dma_start(zv[:, 8 * c:8 * c + 8, :], xr[:, 8 * c:8 * c + 8, :]).then_inc(s["l_x"], 16)
            for t, src in ((xwq[:, :], xWq), (xwk[:, :], xWk), (xwv[:, :], xWv),
                           (xtwc[:, :], xtw.partition_broadcast(128))):
                sp.dma_start(t, src).then_inc(s["l_xw"], 16)
            sp.dma_start(xwo[:, :], xWo).then_inc(s["l_xw"], 16)

            def load_qk(layer):
                w = Wqkv[layer, :, :]
                wait(sp, "p_qk", 4 * B * layer)
                sp.dma_start(wqkv[:, 0:2 * INNER], w[:, 0:2 * INNER]).then_inc(s["l_wqk"], 16)
                wait(sp, "d_rot", 4 * B * layer)
                if layer == 0:
                    sp.wait_ge(s["u_rotq"], 4)
                sp.dma_start(rot[:, :], rot_all[:, layer, :]).then_inc(s["l_rot"], 16)

            def load_v(layer):
                w = Wqkv[layer, :, :]
                wait(sp, "p_v", 2 * B * layer)
                sp.dma_start(wqkv[:, 2 * INNER:3 * INNER], w[:, 2 * INNER:3 * INNER]).then_inc(s["l_wv"], 16)

            def load_o(layer):
                wait(sp, "p_y", B * layer)
                w = Wo[layer, :, :].rearrange("(m i e d) n -> i d m e n", i=2, e=2, d=DH)
                for i in range(2):
                    for e in range(2):
                        sp.dma_start(wo[64 * i:64 * i + 64, e::2, :], w[i, :, :, e, :]).then_inc(s["l_wo"], 16)

            def load_ffn(layer):
                done = B * layer
                wait(sp, "a_gelu", done)
                wait(sp, "d_h", done)
                for o, src in ((0, lng), (1, lnb)):
                    sp.dma_start(gb[:, o:o + 1], src[layer, :].rearrange("(p o) -> p o", o=1)).then_inc(s["l_gb"], 16)
                for h in range(2):
                    for c, (o, m) in enumerate(FCH):
                        src = b1[layer, h * FF + o:h * FF + o + m].rearrange("(p o) -> p o", o=1)
                        sp.dma_start(b1c[0:m, 3 * h + c:3 * h + c + 1], src).then_inc(s["l_gb"], 16)
                wait(sp, "p_a", done)
                sp.dma_start(w1[:, :], W1[layer, :, :]).then_inc(s["l_w1"], 16)
                wait(sp, "p_y2", done)
                for c, (o, m) in enumerate(FCH):
                    sp.dma_start(w2[0:m, c, :], W2[layer, o:o + m, :]).then_inc(s["l_w2"], 16)
                wait(sp, "g_zmb", done)
                sp.dma_start(b2r[:, :], b2[layer, :].partition_broadcast(128)).then_inc(s["l_b2"], 16)

            def shift_v(u, par):
                for e in range(2):
                    wait(sp, "a_v", count(2, u, e + 1))
                    wait(sp, "p_AV", count(2, u - 2, 2))
                    r = slice(64 * e, 64 * e + 64)
                    for j in range(3):
                        sp.dma_start(vs[r, par, j, :], vt[32 * j:32 * j + 64, par, e, :]).then_inc(s[f"l_v{par}"], 16)

            sp.dma_start(qks[:, 0, :], qs.rearrange("l d -> (l d)").partition_broadcast(128)).then_inc(s["l_qks"], 16)
            sp.dma_start(qks[:, 1, :], ks.rearrange("l d -> (l d)").partition_broadcast(128)).then_inc(s["l_qks"], 16)

            for b in range(B):
                if b >= 2:
                    sp.wait_ge(s["x_A1"], b - 1)
                sp.dma_start(ctxb[:, b % 2, :], ctx[b, :, :]).then_inc(s[f"l_ctx{b % 2}"], 16)
                if b == 1:
                    load_qk(0)
                    load_v(0)
                    load_o(0)
                    load_ffn(0)
            for layer in range(DEPTH):
                first = B * layer + 2
                if layer == 0:
                    shift_v(0, 0)
                    shift_v(1, 1)
                with sp.Fori(0, (B - 6) // 2) as i:
                    for k in range(2):
                        shift_v(i * 2 + (first + k), k)
                shift_v(B * layer + B - 4, 0)
                if layer + 1 < DEPTH:
                    load_qk(layer + 1)
                for k in range(3):
                    shift_v(B * layer + B - 3 + k, (1 + k) % 2)
                if layer + 1 < DEPTH:
                    load_v(layer + 1)
                    shift_v(B * layer + B, 0)
                    load_o(layer + 1)
                    shift_v(B * layer + B + 1, 1)
                    load_ffn(layer + 1)
            ov = out.rearrange("b s e -> s b e")
            for c in range(8):
                sp.wait_ge(s["d_out"], c + 1)
                sp.dma_start(ov[:, 4 * c:4 * c + 4, :], x1v[:, 4 * c:4 * c + 4, :]).then_inc(s["out_done"], 16)
            sp.wait_ge(s["out_done"], 128)

        @block.gpsimd
        def _(pool):
            g = nc.gpsimd
            g.memset(half_neg[:, :], -0.5).then_inc(s["u_negh"], 1)
            g.memset(kz[:, :, :, :], 0.0).then_inc(s["u_kz"], 1)
            g.memset(pz[:, :, :, :], 0.0).then_inc(s["u_kz"], 1)
            g.memset(ones[:, :], 1.0).then_inc(s["u_ones"], 1)
            g.memset(vaug[:, :, :, :], 0.0).then_inc(s["u_vz"], 1)
            pool.wait_ge(s["u_vz"], 1)
            g.memset(zsT[64:128, :, 0:1], 0.0).then_inc(s["u_zs"], 1)
            pool.wait_ge(s["u_zs"], 1)
            g.memset(vaug[:, :, :, XD:XD + 1], 1.0).then_inc(s["u_v1"], 1)
            pool.wait_ge(s["l_cst"], 16)
            pool.wait_ge(s["l_qks"], 32)
            for k in range(2):
                sc = qks[:, k, :].rearrange("p (l d) -> p l d", l=DEPTH)
                for c in range(2):
                    o = 128 * k + 64 * c
                    g.tensor_tensor(rot_all[:, :, o:o + 64], sc,
                                    rotc[:, o:o + 64].unsqueeze(1).to_broadcast([128, DEPTH, DH]),
                                    ALU.mult).then_inc(s["u_rotq"], 1)
            pool.wait_ge(s["u_ve"], 1)
            pool.wait_ge(s["u_negh"], 1)
            for b0, b1_ in ((0, 4), (4, B)):
                g.tensor_tensor(rstd0[:, b0:b1_], ve0[:, b0:b1_], half_neg[:, b0:b1_], ALU.pow)\
                    .then_inc(s["u_rstd"], 1)

            def xslot(n, k):
                Bt, B_on = part(n, 1, B)
                D, D_on = part(n, 3, B)
                pB = (k - 1) % 2
                if B_on:
                    for j in range(2):
                        wait(pool, "x_max", count(2, Bt, j + 1, B))
                        for i in range(2):
                            hh = 8 * j + 4 * i
                            pr = XP[:, pB, 128 * hh:128 * hh + 512].rearrange("p (h q) -> p h q", q=S)
                            g.tensor_tensor(pr, pr, xmax[:, hh:hh + 4].unsqueeze(2).to_broadcast([128, 4, S]),
                                            ALU.subtract).then_inc(s["x_sub"], 1)
                if D_on:
                    wait(pool, "x_ve", count(1, D, 1, B))
                    g.tensor_tensor(rstd[:, 0:1], ve[:, 0:1], half_neg[:, 0:1], ALU.pow).then_inc(s["x_rstd"], 1)

            xslots(pool, xslot)

            def slot(n, k):
                z2, z_on = part(n, -2)
                a, a_on = part(n, 0)
                m, m_on = part(n, 1)
                d, d_on = part(n, 4)
                pa, pm, pd = k % 2, (k - 1) % 2, k % 2

                if d_on:
                    wait(pool, "d_ve", count(1, d, 1))
                    g.tensor_tensor(rstd[:, pd:pd + 1], ve[:, pd:pd + 1], half_neg[:, 0:1],
                                    ALU.pow).then_inc(s["g_rstd"], 1)
                if m_on:
                    wait(pool, "g_pow", count(1, m, 1))
                    for j in range(4):
                        wait(pool, "g_add", count(4, m, j + 1))
                        q3 = qk[:, pm, 512 * j:512 * j + 512].rearrange("p (h d) -> p h d", d=DH)
                        r3 = rn[:, pm, 8 * j:8 * j + 8].unsqueeze(2).to_broadcast([128, 8, DH])
                        g.tensor_tensor(q3, q3, r3, ALU.mult).then_inc(s["g_qk"], 1)
                if a_on:
                    for j in range(4):
                        wait(pool, "d_rot", count(4, a, j + 1))
                        wait(pool, "p_tr", count(4, a - 2, j + 1))
                        c = slice(512 * j, 512 * j + 512)
                        o = qk[:, pa, c].rearrange("p (h c d) -> p h c d", c=2, d=32)
                        i0 = ta[:, c].rearrange("p (h c d) -> p h c d", c=2, d=32)
                        i1 = tb[:, c].rearrange("p (h c d) -> p h c d", c=2, d=32)[:, :, ::-1, :]
                        g.tensor_tensor(o, i0, i1, ALU.add).then_inc(s["g_add"], 1)
                if d_on:
                    wait(pool, "d_zm", count(1, d, 1))
                    wait(pool, "l_b2", 16 * layer_of(d) + 16)
                    wait(pool, "z_ready", count(1, d - 2, 1) + B if not (isinstance(d, int) and d < 2) else 0)
                    g.tensor_tensor(zmb[:, pd, :], zm[:, pd, :], b2r[:, :], ALU.add).then_inc(s["g_zmb"], 1)
                if z_on:
                    wait(pool, "z_ready", z2 + 1)
                    wait(pool, "p_zT", count(1, z2 - 2, 1))
                    g.tensor_copy(zcur[:, k % 2, :], z_sb[:, cols(z2)]).then_inc(s["g_z"], 1)
                if a_on:
                    wait(pool, "d_ss", count(1, a, 1))
                    wait(pool, "g_qk", count(4, a - 2, 4))
                    g.tensor_tensor(rn[:, pa, :], ss[:, pa, :], half_neg[:, :], ALU.pow).then_inc(s["g_pow"], 1)

            slots(pool, slot)

        @block.scalar
        def _(act):
            a_ = nc.scalar
            act.preload_act_table_set("natural_log_exp_and_others")
            act.wait_ge(s["u_dmT"], 1)
            a_.activation(dmT[:, :, :].rearrange("p c b -> p (c b)"), bank[6][:, 0:64], ACT.Copy).then_inc(s["u_dmc"], 1)
            act.wait_ge(s["u_ct"], 1)
            a_.activation(ctT[:, :], bank[6][:, 64:96], ACT.Copy).then_inc(s["u_ctc"], 1)

            def xslot(n, k):
                A, A_on = part(n, 0, B)
                Bt, B_on = part(n, 1, B)
                C, C_on = part(n, 2, B)
                D, D_on = part(n, 3, B)
                pA, pB = k % 2, (k - 1) % 2
                if A_on:
                    wait(act, "x_A1", count(1, A, 1, B))
                    wait(act, "x_A2", count(1, A - 2, 1, B))
                    a_.activation(cxT[:, pA, :], bank[6][:, 0:256], ACT.Copy).then_inc(s["x_cxT"], 1)
                if D_on:
                    wait(act, "x_aT", count(1, D, 1, B))
                    wait(act, "x_y", count(1, D - 1, 1, B))
                    a_.activation(attnT[:, :], bank[7][:, 0:128], ACT.Copy).then_inc(s["x_aTc"], 1)
                if C_on:
                    for j in range(4):
                        wait(act, "x_PT", count(4, C, j + 1, B))
                        wait(act, "x_O", count(1, C - 1, 1, B))
                        a_.activation(XPT[:, 4 * j:4 * j + 4, :],
                                      bank[4 + j % 2][:, :].rearrange("p (h q) -> p h q", h=4),
                                      ACT.Copy).then_inc(s["x_PTc"], 1)
                if A_on:
                    wait(act, "x_dabs", count(3, A, 3, B))
                    wait(act, "x_bias", count(1, A - 1, 1, B))
                    a_.activation(lnt[:, :], dabs[:, :], ACT.Ln, bias=1.0).then_inc(s["x_ln"], 1)
                    wait(act, "x_A2", count(1, A, 1, B))
                    wait(act, "x_S", count(4, A - 2, 4, B))
                    a_.activation(qT[:, pA, :], bank[6][:, 0:128], ACT.Copy, scale=XSCALE).then_inc(s["x_q"], 1)
                if C_on:
                    wait(act, "x_O", count(1, C, 1, B))
                    wait(act, "x_OT", count(1, C - 1, 1, B))
                    a_.activation(XO, bank[7][:, :], ACT.Copy).then_inc(s["x_Oc"], 1)
                if B_on:
                    for j in range(2):
                        wait(act, "x_sub", count(4, Bt, 2 * j + 2, B))
                        pr = XP[:, pB, 1024 * j:1024 * j + 1024]
                        a_.activation(pr, pr, ACT.Exp).then_inc(s["x_exp"], 1)

            xslots(act, xslot)

            def slot(n, k):
                zu, z_on = part(n, -1)
                a, a_on = part(n, 0)
                b, b_on = part(n, 2)
                c, c_on = part(n, 3)
                d, d_on = part(n, 4)
                pb = k % 2

                def spread(tile, j, src, name):
                    if isinstance(n, int):
                        act.wait_ge(s["u_kz"], 2)
                    for e in range(2):
                        r = slice(64 * e, 64 * e + 64)
                        ins = a_.activation(tile[r, 4 * j:4 * j + 4, e, :], src[r, :, :], ACT.Copy)
                    ins.then_inc(s[name], 1)

                def square(j):
                    wait(act, "p_qk", count(4, a, j + 1))
                    wait(act, "d_ss", count(1, a - 1, 1))
                    a_.activation(sq[:, 512 * j:512 * j + 512], bank[j % 2][:, :], ACT.Square)\
                        .then_inc(s["a_sq"], 1)

                def copy_T(j):
                    wait(act, "p_tr", count(4, b, j + 1))
                    wait(act, "p_S", count(2, b - 1, 2))
                    src = bank[4 + j % 2][:, :].rearrange("p (h q) -> p h q", h=4)
                    if j < 2:
                        a_.activation(qT2[:, 4 * j:4 * j + 4, :], src, ACT.Copy).then_inc(s["a_tr"], 1)
                    else:
                        spread(kz, j - 2, src, "a_tr")

                def copy_v(e):
                    wait(act, "p_v", count(2, b, e + 1))
                    wait(act, f"l_v{pb}", 96 * ((b - 2) // 2) + 96 if isinstance(b, int) else (b >> 1) * 96)
                    a_.activation(vt[:, pb, e, :], bank[e][:, :], ACT.Copy).then_inc(s["a_v"], 1)

                def copy_o(j):
                    wait(act, "p_AV", count(2, c, j + 1))
                    wait(act, "p_y", count(1, c - 1, 1))
                    a_.activation(oT[:, 4 * j:4 * j + 4, :],
                                  bank[4 + j][:, :].rearrange("p (h q) -> p h q", h=4),
                                  ACT.Copy).then_inc(s["a_AV"], 1)

                if a_on:
                    square(0)
                if b_on:
                    copy_T(0)
                    copy_T(1)
                if a_on:
                    square(1)
                if b_on:
                    copy_T(2)
                    copy_T(3)
                if a_on:
                    square(2)
                if z_on:
                    wait(act, "p_zT", count(1, zu, 1))
                    wait(act, "p_v", count(2, zu - 4, 2))
                    if isinstance(zu, int) and zu < 4:
                        wait(act, "u_zs", 1)
                    t = zsT[:, (k + 1) % 4, :]
                    a_.activation(t[0:64, :], bank[7][0:64, 0:128], ACT.Copy).then_inc(s["a_zs"], 1)
                    a_.activation(t[64:128, 1:128], bank[7][64:128, 0:127], ACT.Copy).then_inc(s["a_zs"], 1)
                if c_on:
                    for j in range(2):
                        wait(act, "p_PT", count(2, c, j + 1))
                        wait(act, "p_AV", count(2, c - 1, 2))
                        spread(pz, j, bank[4 + j][:, :].rearrange("p (h q) -> p h q", h=4), "a_PT")
                if d_on:
                    wait(act, "p_znT", count(1, d, 1))
                    wait(act, "l_gb", 128 * layer_of(d) + 128)
                    wait(act, "p_a", count(1, d - 1, 1))
                    a_.activation(znT[:, :], bank[6][:, 0:128], ACT.Identity, scale=gb[:, 0:1], bias=gb[:, 1:2])\
                        .then_inc(s["a_zn"], 1)
                act.preload_act_table_set("gelu_and_others")
                if a_on:
                    square(3)
                if d_on:
                    wait(act, "p_gate", count(1, d, 1))
                    wait(act, "d_h", count(1, d - 1, 1))
                    for j, (_, m) in enumerate(FCH):
                        ins = a_.activation(gl[0:m, j, :], bank[7][0:m, 128 * j:128 * j + 128], ACT.Gelu,
                                            bias=b1c[0:m, 3 + j:4 + j])
                    ins.then_inc(s["a_gelu"], 1)
                act.preload_act_table_set("natural_log_exp_and_others")
                if b_on:
                    wait(act, "d_sub", count(2, b, 2))
                    a_.activation(P[:, pb, :], P[:, pb, :], ACT.Exp).then_inc(s["a_exp"], 1)
                if b_on:
                    copy_v(0)
                if c_on:
                    copy_o(0)
                    copy_o(1)
                if b_on:
                    copy_v(1)

            slots(act, slot)

        @block.vector
        def _(dve):
            v_ = nc.vector
            dve.wait_ge(s["l_cst"], 16)
            v_.tensor_copy(identb[:, :], ident).then_inc(s["u_bf"], 1)
            v_.tensor_copy(maskb[:, :], cst[:, C_MASK:C_MASK + 64]).then_inc(s["u_bf"], 1)
            dve.wait_ge(s["u_dmc"], 1)
            v_.tensor_scalar(dmT[:, 1, :], dmT[:, 1, :], -1.0, 1e9, ALU.add, ALU.mult).then_inc(s["u_dmc"], 1)
            dve.wait_ge(s["l_x"], 64)
            for b in range(B):
                v_.bn_stats(stx[:, 6 * b:6 * b + 6], zv[:, b, :]).then_inc(s["u_st"], 1)
            dve.wait_ge(s["u_st"], B)
            st = stx[:, :].rearrange("p (b c) -> p b c", c=6)
            v_.tensor_tensor(mean0[:, :], st[:, :, 1], st[:, :, 4], ALU.add).then_inc(s["u_ag"], 1)
            v_.tensor_tensor(dif0[:, :], st[:, :, 1], st[:, :, 4], ALU.subtract).then_inc(s["u_ag"], 1)
            v_.tensor_tensor(ve0[:, :], st[:, :, 2], st[:, :, 5], ALU.add).then_inc(s["u_ag"], 1)
            dve.wait_ge(s["u_ag"], 3)
            v_.tensor_scalar(mean0[:, :], mean0[:, :], 0.5, None, ALU.mult).then_inc(s["u_ag"], 1)
            v_.tensor_tensor(dif0[:, :], dif0[:, :], dif0[:, :], ALU.mult).then_inc(s["u_ag"], 1)
            v_.tensor_scalar(ve0[:, :], ve0[:, :], 1.0 / E, LN_EPS, ALU.mult, ALU.add).then_inc(s["u_ag"], 1)
            dve.wait_ge(s["u_ag"], 6)
            v_.scalar_tensor_tensor(ve0[:, :], dif0[:, :], 0.25, ve0[:, :], ALU.mult, ALU.add).then_inc(s["u_ve"], 1)
            dve.wait_ge(s["l_xw"], 80)
            v_.tensor_copy(xwkr[:, :].rearrange("p (g r d) -> p g r d", g=XG, r=XR),
                           xwk[:, :].rearrange("p (g d) -> p g d", g=XG).unsqueeze(2).to_broadcast([128, XG, XR, XD]))\
                .then_inc(s["u_wkr"], 1)
            dve.wait_ge(s["u_dmc"], 2)
            dve.wait_ge(s["u_ctc"], 1)
            dmf = dmT[:, :, :].rearrange("p c b -> p (c b)")

            def rows(A, pA):
                wait(dve, "x_A1", count(1, A - 2, 1, B))
                if isinstance(A, int) and A <= 4:
                    dve.wait_ge(s["u_rstd"], 1 if A < 4 else 2)
                v_.tensor_scalar(xn[:, pA, :], z_sb[:, bass.ds(A * E, E)], mean0[:, bass.ds(A, 1)],
                                 rstd0[:, bass.ds(A, 1)], ALU.subtract, ALU.mult).then_inc(s["x_xn"], 1)
                v_.tensor_scalar(td[:, pA, 0:S], tri, dmf[:, bass.ds(A, 1)], None, ALU.mult)\
                    .then_inc(s["x_td"], 1)
                v_.tensor_scalar(td[:, pA, S:2 * S], ident, dmf[:, bass.ds(A + B, 1)], None, ALU.mult)\
                    .then_inc(s["x_td"], 1)

            rows(0, 0)

            def xslot(n, k):
                A1, A1_on = part(n, -1, B)
                A, A_on = part(n, 0, B)
                Bt, B_on = part(n, 1, B)
                D, D_on = part(n, 3, B)
                pA, pB = k % 2, (k - 1) % 2
                xc = bass.ds(D * E, E)
                def add_bias(gr):
                    wait(dve, "x_S", count(4, Bt, gr + 1, B))
                    if gr == 0:
                        wait(dve, "x_PT", count(4, Bt - 2, 4, B))
                        wait(dve, "x_bias", count(1, Bt, 1, B))
                    v_.tensor_tensor(XP[:, pB, 512 * gr:512 * gr + 512].rearrange("p (h q) -> p h q", q=S),
                                     bank[gr][:, :].rearrange("p (h q) -> p h q", q=S),
                                     bias[:, pB, :].unsqueeze(1).to_broadcast([128, 4, S]), ALU.add)\
                        .then_inc(s["x_add"], 1)

                def maximum(j):
                    pr = XP[:, pB, 1024 * j:1024 * j + 1024].rearrange("p (h q) -> p h q", q=S)
                    wait(dve, "x_add", count(4, Bt, 2 * j + 2, B))
                    wait(dve, "x_sub", count(4, Bt - 1, 2 * j + 2, B))
                    v_.tensor_reduce(xmax[:, 8 * j:8 * j + 8], pr, AX.X, ALU.max).then_inc(s["x_max"], 1)

                if B_on:
                    add_bias(0)
                if D_on:
                    wait(dve, "x_OT", count(1, D, 1, B))
                    o4 = bank[7][:, :].rearrange("p (r g d) -> p r g d", r=XR, g=XG)
                    v_.reciprocal(xrs[:, :].rearrange("p (g r) -> p r g", g=XG), o4[:, :, :, XD]).then_inc(s["x_rs"], 1)
                if B_on:
                    add_bias(1)
                if D_on:
                    wait(dve, "x_rs", count(1, D, 1, B))
                    wait(dve, "x_aT", count(1, D - 1, 1, B))
                    at = attn[:, :, :].rearrange("p (g r) d -> p r g d", g=XG)
                    rs = xrs[:, :].rearrange("p (g r) -> p r g", g=XG)
                    for r in range(XR):
                        ins = v_.tensor_tensor(at[:, r, :, :], o4[:, r, :, 0:XD],
                                               rs[:, r, :].unsqueeze(2).to_broadcast([128, XG, XD]), ALU.mult)
                    ins.then_inc(s["x_attn"], 1)
                if A_on:
                    wait(dve, "x_A1", count(1, A, 1, B))
                    wait(dve, "x_ln", count(1, A - 1, 1, B))
                    wait(dve, "x_cxT", count(1, A, 1, B))
                    wait(dve, "x_bias", count(1, A - 1, 1, B))
                    v_.tensor_copy(mbr[:, :], bank[6][:, 384:512]).then_inc(s["x_dabs"], 1)
                    v_.tensor_scalar(dif[:, :], bank[6][:, 256:384], ctT[:, bass.ds(A, 1)], None,
                                     ALU.subtract).then_inc(s["x_dabs"], 1)
                    wait(dve, "x_dabs", count(3, A, 2, B))
                    v_.scalar_tensor_tensor(dabs[:, :], dif[:, :], -1.0, dif[:, :], ALU.mult, ALU.max)\
                        .then_inc(s["x_dabs"], 1)
                if B_on:
                    add_bias(2)
                    maximum(0)
                    add_bias(3)
                    maximum(1)
                if D_on:
                    wait(dve, "x_y", count(1, D, 1, B))
                    v_.tensor_tensor(x1cur[:, :], bank[4][:, 0:128], z_sb[:, xc], ALU.add).then_inc(s["x_x1"], 1)
                if D_on:
                    wait(dve, "x_x1", count(1, D, 1, B))
                    v_.bn_stats(stats[:, 0:6], x1cur[:, :]).then_inc(s["x_bn"], 1)
                if A_on:
                    wait(dve, "x_ln", count(1, A, 1, B))
                    wait(dve, "x_dabs", count(3, A, 3, B))
                    v_.scalar_tensor_tensor(bias[:, pA, :], lnt[:, :], xtwc[:, 0:1], mbr[:, :], ALU.mult, ALU.add)\
                        .then_inc(s["x_bias"], 1)
                if D_on:
                    wait(dve, "x_bn", count(1, D, 1, B))
                    v_.tensor_copy(x1_sb[:, xc], x1cur[:, :]).then_inc(s["x_store"], 1)
                    v_.bn_aggr(mv[:, :], stats[:, 0:6]).then_inc(s["x_agg"], 1)
                if A_on:
                    wait(dve, "x_A2", count(1, A, 1, B))
                    wait(dve, "x_q", count(1, A, 1, B))
                    wait(dve, "x_S", count(4, A - 2, 4, B))
                    v_.tensor_tensor(kblk[:, pA, :].rearrange("p (r t) -> p r t", r=XR),
                                     bank[6][:, 128:256].unsqueeze(1).to_broadcast([128, XR, S]),
                                     blk.unsqueeze(2).to_broadcast([128, XR, S]), ALU.mult).then_inc(s["x_kblk"], 1)
                if D_on:
                    wait(dve, "x_agg", count(1, D, 1, B))
                    v_.tensor_scalar(ve[:, 0:1], mv[:, 1:2], LN_EPS, None, ALU.add).then_inc(s["x_ve"], 1)
                if A1_on:
                    rows(A1, (k + 1) % 2)
                if A_on:
                    wait(dve, "x_O", count(1, A - 2, 1, B))
                    wait(dve, "u_v1", 1)
                    v_.tensor_copy(vaug[:, pA, :, 0:XD], bank[6][:, 256:288].rearrange("p (g d) -> p g d", g=XG))\
                        .then_inc(s["x_vaug"], 1)
                if D_on:
                    wait(dve, "x_rstd", count(1, D, 1, B))
                    v_.tensor_scalar(z_sb[:, xc], x1cur[:, :], mv[:, 0:1], rstd[:, 0:1], ALU.subtract, ALU.mult)\
                        .then_inc(s["z_ready"], 1)

            xslots(dve, xslot)

            def slot(n, k):
                a, a_on = part(n, 0)
                b, b_on = part(n, 2)
                c, c_on = part(n, 3)
                d, d_on = part(n, 4)
                pa, pb, pd = k % 2, k % 2, k % 2

                def rotary(j):
                    wait(dve, "a_sq", count(4, a, j + 1))
                    wait(dve, "g_add", count(4, a - 1, j + 1))
                    if j == 0:
                        wait(dve, "l_rot", 16 * layer_of(a) + 16)
                    o = 128 * (j // 2)
                    src = bank[j % 2][:, :].rearrange("p (h d) -> p h d", d=DH)
                    for t, r in ((ta, rot[:, o:o + 64]), (tb, rot[:, o + 64:o + 128])):
                        ins = v_.tensor_tensor(t[:, 512 * j:512 * j + 512].rearrange("p (h d) -> p h d", d=DH), src,
                                               r.unsqueeze(1).to_broadcast([128, 8, DH]), ALU.mult)
                    ins.then_inc(s["d_rot"], 1)

                if d_on:
                    wait(dve, "p_y", count(1, d, 1))
                    wait(dve, "p_zsh", count(1, d - 2, 1))
                    wait(dve, "g_zmb", count(1, d - 2, 1))
                    v_.tensor_tensor(zm[:, pd, :], bank[7][:, 384:512], z_sb[:, cols(d)], ALU.add)\
                        .then_inc(s["d_zm"], 1)
                if a_on:
                    rotary(0)
                if d_on:
                    wait(dve, "p_zsh", count(1, d, 1))
                    v_.bn_stats(stats[:, 0:6], bank[6][:, 0:128]).then_inc(s["d_bn"], 1)
                    wait(dve, "d_bn", count(1, d, 1))
                    dve.nop(nofuse=True)
                    v_.bn_aggr(mv[:, :], stats[:, 0:6]).then_inc(s["d_agg"], 1)
                    wait(dve, "d_agg", count(1, d, 1))
                    v_.tensor_scalar(ve[:, pd:pd + 1], mv[:, 1:2], LN_EPS, None, ALU.add).then_inc(s["d_ve"], 1)
                if a_on:
                    rotary(1)
                if d_on:
                    wait(dve, "g_rstd", count(1, d, 1))
                    wait(dve, "p_znT", count(1, d - 1, 1))
                    v_.tensor_scalar(zn[:, :], bank[6][:, 0:128], mv[:, 0:1], rstd[:, pd:pd + 1],
                                     ALU.subtract, ALU.mult).then_inc(s["d_zn"], 1)
                if a_on:
                    rotary(2)
                if b_on:
                    for j in range(2):
                        wait(dve, "p_S", count(2, b, j + 1))
                        v_.tensor_reduce(rowmax[:, 8 * j:8 * j + 8], SC[j][:, :].rearrange("p (h t) -> p h t", t=DH),
                                         AX.X, ALU.max).then_inc(s["d_max"], 1)
                    wait(dve, "p_PT", count(2, b - 2, 2))
                    for j in range(2):
                        wait(dve, "d_max", count(2, b, j + 1))
                        v_.tensor_tensor(P[:, pb, 512 * j:512 * j + 512].rearrange("p (h t) -> p h t", t=DH),
                                         SC[j][:, :].rearrange("p (h t) -> p h t", t=DH),
                                         rowmax[:, 8 * j:8 * j + 8].unsqueeze(2).to_broadcast([128, PAIRS, DH]),
                                         ALU.subtract).then_inc(s["d_sub"], 1)
                if a_on:
                    rotary(3)
                if d_on:
                    wait(dve, "p_a", count(1, d, 1))
                    wait(dve, "a_gelu", count(1, d, 1))
                    wait(dve, "p_y2", count(1, d - 1, 1))
                    for j, (_, m) in enumerate(FCH):
                        ins = v_.scalar_tensor_tensor(hT[0:m, j, :], bank[6][0:m, 128 * j:128 * j + 128],
                                                      b1c[0:m, j:j + 1], gl[0:m, j, :], ALU.add, ALU.mult)
                    ins.then_inc(s["d_h"], 1)
                if a_on:
                    wait(dve, "g_pow", count(1, a - 2, 1))
                    v_.tensor_reduce(ss[:, pa, :], sq[:, :].rearrange("p (h d) -> p h d", d=DH), AX.X, ALU.add)\
                        .then_inc(s["d_sumsq"], 1)
                    wait(dve, "d_sumsq", count(1, a, 1))
                    v_.tensor_scalar(ss[:, pa, :], ss[:, pa, :], NORM_MIN2, None, ALU.max).then_inc(s["d_ss"], 1)
                if b_on:
                    wait(dve, "a_exp", count(1, b, 1))
                    pr = P[:, pb, :].rearrange("p (h t) -> p h t", t=DH)
                    v_.tensor_reduce(rowsum[:, 0, :], pr, AX.X, ALU.add).then_inc(s["d_sum"], 1)
                    wait(dve, "d_sum", count(1, b, 1))
                    v_.reciprocal(rowsum[:, 1, :], rowsum[:, 0, :]).then_inc(s["d_rec"], 1)
                    wait(dve, "d_rec", count(1, b, 1))
                    v_.tensor_tensor(pr, pr, rowsum[:, 1, :].unsqueeze(2).to_broadcast([128, HEADS, DH]),
                                     ALU.mult).then_inc(s["d_P"], 1)
                if d_on:
                    wait(dve, "p_y2", count(1, d, 1))
                    wait(dve, "g_zmb", count(1, d, 1))
                    v_.tensor_tensor(z_sb[:, cols(d)], bank[6][:, 384:512], zmb[:, pd, :], ALU.add)\
                        .then_inc(s["z_ready"], 1)

            slots(dve, slot)
            dve.wait_ge(s["z_ready"], B + UNITS)
            dve.wait_ge(s["x_store"], B)
            for c in range(8):
                cc = slice(512 * c, 512 * c + 512)
                v_.tensor_tensor(x1_sb[:, cc], x1_sb[:, cc], z_sb[:, cc], ALU.add).then_inc(s["d_out"], 1)

        @block.tensor
        def _(pe):
            t_ = nc.tensor
            pe.wait_ge(s["l_cst"], 16)
            pe.wait_ge(s["l_dm"], 32)
            t_.transpose(bank[6][:, 0:32], dm[:, 0, :], ident[0:32, 0:32])
            t_.transpose(bank[6][:, 32:64], dm[:, 1, :], ident[0:32, 0:32]).then_inc(s["u_dmT"], 1)
            pe.wait_ge(s["u_dmc"], 1)
            t_.matmul(bank[6][:, 64:96], tri, dmT[:, 0, :], start=True, stop=True).then_inc(s["u_ct"], 1)
            pe.wait_ge(s["u_ctc"], 1)
            pe.wait_ge(s["u_ones"], 1)
            pe.wait_ge(s["l_xw"], 80)
            pe.wait_ge(s["u_wkr"], 1)

            def xslot(n, k):
                A, A_on = part(n, 0, B)
                Bt, B_on = part(n, 1, B)
                C, C_on = part(n, 2, B)
                D, D_on = part(n, 3, B)
                pA, pB, pC = k % 2, (k - 1) % 2, k % 2
                def xscores(gr):
                    wait(pe, "x_add", count(4, Bt - 1, gr + 1, B))
                    r = slice(32 * gr, 32 * gr + 32)
                    t_.matmul(bank[gr][:, :], qT[r, pB, :], kblk[r, pB, :], start=True, stop=True)\
                        .then_inc(s["x_S"], 1)

                if B_on:
                    wait(pe, "x_q", count(1, Bt, 1, B))
                    wait(pe, "x_kblk", count(1, Bt, 1, B))
                    xscores(0)
                    xscores(1)
                if D_on:
                    wait(pe, "x_Oc", count(1, D, 1, B))
                    for r in range(XR):
                        ins = t_.transpose(bank[7][:, 128 * r:128 * r + 128], XO[:, 128 * r:128 * r + 128], ident)
                    ins.then_inc(s["x_OT"], 1)
                if A_on:
                    wait(pe, f"l_ctx{pA}", 16 * (A // 2) + 16 if isinstance(A, int) else (A >> 1) * 16 + 16)
                    wait(pe, "x_xn", count(1, A, 1, B))
                    wait(pe, "x_td", count(2, A, 2, B))
                    wait(pe, "x_kblk", count(1, A - 1, 1, B))
                    wait(pe, "x_vaug", count(1, A - 1, 1, B))
                    t_.transpose(bank[6][:, 0:128], ctxb[:, pA, :], ident)
                    t_.transpose(bank[6][:, 128:256], xn[:, pA, :], ident)
                    t_.matmul(bank[6][:, 256:512], ones[:, :], td[:, pA, :], start=True, stop=True)\
                        .then_inc(s["x_A1"], 1)
                if B_on:
                    xscores(2)
                    xscores(3)
                if D_on:
                    wait(pe, "x_attn", count(1, D, 1, B))
                    t_.transpose(bank[7][:, 0:128], attn[:, :, :].rearrange("p h d -> p (h d)"), ident)\
                        .then_inc(s["x_aT"], 1)
                if C_on:
                    wait(pe, "x_x1", count(1, D - 1, 1, B))
                    for j in range(4):
                        wait(pe, "x_exp", count(2, C, j // 2 + 1, B))
                        wait(pe, "x_PTc", count(4, C, j - 1, B) if j >= 2 else count(4, C - 1, j + 3, B))
                        for h in range(4):
                            hh = 4 * j + h
                            ins = t_.transpose(bank[4 + j % 2][:, 128 * h:128 * h + 128],
                                               XP[:, pC, 128 * hh:128 * hh + 128], ident)
                        ins.then_inc(s["x_PT"], 1)
                if A_on:
                    wait(pe, "x_cxT", count(1, A, 1, B))
                    wait(pe, "x_dabs", count(3, A, 2, B))
                    t_.matmul(bank[6][:, 0:128], xwq[:, :], cxT[:, pA, S:2 * S], start=True, stop=True)
                    t_.matmul(bank[6][:, 128:256], xwkr[:, :], cxT[:, pA, 0:S], start=True, stop=True)
                    t_.matmul(bank[6][:, 256:288], cxT[:, pA, 0:S], xwv[:, :], start=True, stop=True)\
                        .then_inc(s["x_A2"], 1)
                if D_on:
                    wait(pe, "x_aTc", count(1, D, 1, B))
                    wait(pe, "x_PTc", count(4, C, 3, B))
                    t_.matmul(bank[4][:, 0:128], attnT[:, :], xwo[:, :], start=True, stop=True)\
                        .then_inc(s["x_y"], 1)
                if C_on:
                    wait(pe, "x_PTc", count(4, C, 4, B))
                    wait(pe, "x_vaug", count(1, C, 1, B))
                    wait(pe, "x_aTc", count(1, D, 1, B))
                    for gr in range(XG):
                        ins = t_.matmul(bank[7][32 * gr:32 * gr + 32, :], vaug[:, pC, gr, :],
                                        XPT[:, 4 * gr:4 * gr + 4, :], start=True, stop=True)
                    ins.then_inc(s["x_O"], 1)

            xslots(pe, xslot)
            pe.wait_ge(s["u_bf"], 2)
            pe.wait_ge(s["x_x1"], B)

            def slot(n, k):
                zu, z_on = part(n, -1)
                a, a_on = part(n, 0)
                b, b_on = part(n, 2)
                c, c_on = part(n, 3)
                d, d_on = part(n, 4)
                pb, pc, pd = k % 2, (k - 3) % 2, k % 2

                def proj_qk(j):
                    if j == 0:
                        wait(pe, "a_zs", count(2, a, 2))
                        wait(pe, "l_wqk", 16 * layer_of(a) + 16)
                    if j < 2:
                        edge(pe, n, "d_rot", count(4, a - 1, j + 3))
                        wait(pe, "a_v", count(2, b - 1, j + 1))
                    else:
                        wait(pe, "d_rot", count(4, a, j - 1))
                    t_.matmul(bank[j % 2][:, :], zsT[:, k % 4, :], wqkv[:, 512 * j:512 * j + 512],
                              start=True, stop=True).then_inc(s["p_qk"], 1)

                def proj_v(e):
                    if e == 0:
                        wait(pe, "l_wv", 16 * layer_of(b) + 16)
                    wait(pe, "d_rot", count(4, a, e + 3))
                    edge(pe, n, "a_v", count(2, b - 1, e + 1))
                    wv = wqkv[:, 2 * INNER:].rearrange("i (p e d) -> i p e d", e=2, d=DH)
                    t_.matmul(bank[e][:, :], zsT[:, (k + 2) % 4, :], wv[:, :, e, :], start=True, stop=True)\
                        .then_inc(s["p_v"], 1)

                def transpose_qk(j):
                    wait(pe, "g_qk", count(4, b, j + 1))
                    if j < 2:
                        edge(pe, n, "a_tr", count(4, b - 1, j + 3))
                        wait(pe, "a_AV", count(2, c - 1, j + 1))
                    else:
                        wait(pe, "a_tr", count(4, b, j - 1))
                    for p in range(4):
                        ins = t_.transpose(bank[4 + j % 2][:, 128 * p:128 * p + 128],
                                           qk[:, pb, 512 * j + 128 * p:512 * j + 128 * p + 128], ident)
                    ins.then_inc(s["p_tr"], 1)

                def attend(j):
                    if j == 0:
                        wait(pe, f"l_v{pc}", 96 * (c // 2) + 96 if isinstance(c, int) else (c >> 1) * 96 + 96)
                    wait(pe, "a_PT", count(2, c, j + 1))
                    for m in range(2):
                        for i in range(2):
                            hp = 4 * j + 2 * m + i
                            hc = slice(64 * hp, 64 * hp + 64)
                            o = bank[4 + j][64 * i:64 * i + 64, 256 * m:256 * m + 256]\
                                .rearrange("p (e q) -> p e q", e=2)
                            for w, (q0, nq) in enumerate(((0, 64), (64, 32), (96, 32))):
                                ins = t_.matmul(o[:, :, q0:q0 + nq], vs[:, pc, w, hc], pz[:, hp, :, q0:q0 + nq],
                                                start=True, stop=True)
                    ins.then_inc(s["p_AV"], 1)

                if a_on:
                    proj_qk(0)
                if b_on:
                    transpose_qk(0)
                    transpose_qk(1)
                if d_on:
                    wait(pe, "d_zm", count(1, d, 1))
                    wait(pe, "z_ready", (count(1, d - 1, 1) if isinstance(d, int) else d) + B)
                    t_.matmul(bank[6][:, 0:64], ident, zm[:, pd, 0:64], start=True, stop=True)
                    t_.matmul(bank[6][:, 64:128], shift, zm[:, pd, 64:128], start=True, stop=True)\
                        .then_inc(s["p_zsh"], 1)
                if a_on:
                    proj_qk(1)
                if b_on:
                    transpose_qk(2)
                    transpose_qk(3)
                if a_on:
                    proj_qk(2)
                if z_on:
                    wait(pe, "g_z", count(1, zu, 1))
                    edge(pe, n, "d_zm", count(1, d, 1))
                    edge(pe, n, "a_zs", count(2, zu - 1, 2))
                    t_.transpose(bank[7][:, 0:128], zcur[:, (k + 1) % 2, :], ident).then_inc(s["p_zT"], 1)
                def scores(j):
                    if j == 0:
                        wait(pe, "a_tr", count(4, b, 3))
                    else:
                        edge(pe, n, "a_tr", count(4, b, 4))
                    wait(pe, "d_sub", count(2, b - 1, j + 1))
                    t_.matmul(SC[j][:, :], identb[:, :], maskb[:, :].unsqueeze(1).to_broadcast([128, PAIRS, DH]),
                              start=True, stop=False, skip_group_check=True)
                    for p in range(4 * j, 4 * j + 4):
                        for q0, nq, k0 in ((0, 2 * WIN, 0), (2 * WIN, WIN, WIN), (3 * WIN, WIN, 2 * WIN)):
                            ins = t_.matmul(SC[j][q0:q0 + nq, 128 * (p - 4 * j):128 * (p - 4 * j) + 128],
                                            qT2[:, p, q0:q0 + nq], kz[:, p, :, k0:k0 + 64],
                                            start=False, stop=p % 4 == 3, skip_group_check=True)
                    ins.then_inc(s["p_S"], 1)

                if b_on:
                    scores(0)
                if c_on:
                    for j in range(2):
                        if j == 0:
                            wait(pe, "d_P", count(1, c, 1))
                        if j == 1:
                            wait(pe, "a_tr", count(4, b, 4))
                        edge(pe, n, "a_tr", count(4, b, 3))
                        edge(pe, n, "a_AV", count(2, c - 1, 2))
                        for p in range(4):
                            hp = 4 * j + p
                            ins = t_.transpose(bank[4 + j][:, 128 * p:128 * p + 128],
                                               P[:, pc, 128 * hp:128 * hp + 128], ident)
                        ins.then_inc(s["p_PT"], 1)
                if d_on:
                    wait(pe, "d_zn", count(1, d, 1))
                    t_.transpose(bank[6][:, 0:128], zn[:, :], ident).then_inc(s["p_znT"], 1)
                if b_on:
                    scores(1)
                if a_on:
                    proj_qk(3)
                if d_on:
                    wait(pe, "a_zn", count(1, d, 1))
                    wait(pe, "l_w1", 16 * layer_of(d) + 16)
                    edge(pe, n, "a_zs", count(2, zu, 2))
                    for j, (o, m) in enumerate(FCH):
                        ins = t_.matmul(bank[7][0:m, 128 * j:128 * j + 128], w1[:, FF + o:FF + o + m], znT[:, :],
                                        start=True, stop=True)
                    ins.then_inc(s["p_gate"], 1)
                    for j, (o, m) in enumerate(FCH):
                        ins = t_.matmul(bank[6][0:m, 128 * j:128 * j + 128], w1[:, o:o + m], znT[:, :],
                                        start=True, stop=True)
                    ins.then_inc(s["p_a"], 1)
                if b_on:
                    proj_v(0)
                if c_on:
                    attend(0)
                if c_on:
                    attend(1)
                if b_on:
                    proj_v(1)
                if d_on:
                    wait(pe, "d_h", count(1, d, 1))
                    wait(pe, "l_w2", 48 * layer_of(d) + 48)
                    for j, (_, m) in enumerate(FCH):
                        ins = t_.matmul(bank[6][:, 384:512], hT[0:m, j, :], w2[0:m, j, :], start=j == 0, stop=j == 2)
                    ins.then_inc(s["p_y2"], 1)
                if c_on:
                    wait(pe, "a_AV", count(2, c, 2))
                    wait(pe, "l_wo", 64 * layer_of(c) + 64)
                    edge(pe, n, "a_gelu", count(1, d, 1))
                    edge(pe, n, "a_zs", count(2, zu, 2))
                    for p in range(PAIRS):
                        ins = t_.matmul(bank[7][:, 384:512], oT[:, p, :], wo[:, p, :], start=p == 0,
                                        stop=p == PAIRS - 1)
                    ins.then_inc(s["p_y"], 1)

            slots(pe, slot)


_INS = ['x', 'ctx_1024', 'fside_BxS2_0', 'mask_BxS2_ff1', 'L0_xattn_Wq', 'L0_xattn_Wk', 'L0_xattn_Wv', 'L0_xattn_Wo',
        'L0_xattn_time_bias_weight', 'L0_ffn_Wqkv', 'L0_ffn_q_scale', 'L0_ffn_k_scale', 'L0_ffn_Wo', 'L0_ffn_ln_g',
        'L0_ffn_ln_b', 'L0_ffn_W1', 'L0_ffn_b1', 'L0_ffn_W2', 'L0_ffn_b2']


def kernel(**inputs):
    import concourse.bacc as bacc
    from concourse.bass_utils import run_bass_kernel_spmd

    nc = bacc.Bacc("TRN2", target_bir_lowering=False, num_devices=1)
    arrays, args = {}, []
    for name in _INS:
        a = np.ascontiguousarray(inputs[name])
        if a.ndim == 0 or name == 'L0_xattn_time_bias_weight':
            a = a.reshape(1)
        arrays[name] = a
    arrays["consts"] = constants()
    for name, a in arrays.items():
        args.append(nc.dram_tensor(name, a.shape, mybir.dt.from_np(a.dtype), kind="ExternalInput").ap())
    args.append(nc.dram_tensor("out", (B, S, E), F32, kind="ExternalOutput").ap())
    build(nc, *args)
    r = run_bass_kernel_spmd(nc, [arrays], core_ids=[0])
    return r.results[0]["out"]
```
